# Optimizing a Trainium2 kernel written in Bass

```python
import numpy as np
import jax
import jax.numpy as jnp

def _softmax(x, axis=-1):
    return jax.nn.softmax(x, axis=axis)

def _gelu(x):
    return jax.nn.gelu(x, approximate=True)

def _silu(x):
    return jax.nn.silu(x)

def _sigmoid(x):
    return jax.nn.sigmoid(x)

def _layernorm(x, axis=-1, eps=1e-05):
    m = jnp.mean(x, axis=axis, keepdims=True)
    v = jnp.var(x, axis=axis, keepdims=True)
    return (x - m) / jnp.sqrt(v + eps)

def _scatter_add(tgt, idx, src, axis=0):
    return tgt.at[idx].add(src)

def _segment_sum(src, seg, n):
    return jax.ops.segment_sum(src, seg, n)
kernel_name = 'mk_macaron_d1_jaxref_r8_247ae2'

def setup_inputs(seed: int=0):
    np.random.seed(seed)
    _w = jnp.asarray

    def _L0_attn_setup():
        import jax, jax.numpy as jnp
        import numpy as np
        N_HEAD = 16

        def _phi(x):
            return jax.nn.silu(x) + 1.0
        key = jax.random.key(seed)
        ks = jax.random.split(key, 8)
        B, T, D = (8, 512, 128)
        s = 0.02
        return {'x': jax.random.normal(ks[0], (B, T, D), jnp.float32), 'Wq': jax.random.normal(ks[1], (D, D), jnp.float32) * s, 'bq': jax.random.normal(ks[2], (D,), jnp.float32) * s, 'Wk': jax.random.normal(ks[3], (D, D), jnp.float32) * s, 'Wv': jax.random.normal(ks[4], (D, D), jnp.float32) * s, 'bv': jax.random.normal(ks[5], (D,), jnp.float32) * s, 'Wo': jax.random.normal(ks[6], (D, D), jnp.float32) * s, 'bo': jax.random.normal(ks[7], (D,), jnp.float32) * s}
    _L0_attn_in = _L0_attn_setup()

    def _L0_ffn_setup():
        import jax, jax.numpy as jnp
        import numpy as np
        B, S, H = (2, 256, 128)
        E_ROUTED = 8
        TOP_K = 2
        I = 256
        key = jax.random.key(seed)
        ks = jax.random.split(key, 9)
        s = 0.02
        return {'x': jax.random.normal(ks[0], (B, S, H), dtype=jnp.float32), 'shared_gate': jax.random.normal(ks[1], (I, H), dtype=jnp.float32) * s, 'shared_up': jax.random.normal(ks[2], (I, H), dtype=jnp.float32) * s, 'shared_down': jax.random.normal(ks[3], (H, I), dtype=jnp.float32) * s, 'gate_w': jax.random.normal(ks[4], (E_ROUTED, H, I), dtype=jnp.float32) * s, 'up_w': jax.random.normal(ks[5], (E_ROUTED, H, I), dtype=jnp.float32) * s, 'down_w': jax.random.normal(ks[6], (E_ROUTED, I, H), dtype=jnp.float32) * s, 'router_w': jax.random.normal(ks[7], (E_ROUTED, H), dtype=jnp.float32) * s, 'routing_bias': jnp.zeros((E_ROUTED,), dtype=jnp.float32)}
    _L0_ffn_in = _L0_ffn_setup()
    _d = {'L0_attn_x': _L0_attn_in['x'], 'L0_attn_Wq': _L0_attn_in['Wq'], 'L0_attn_bq': _L0_attn_in['bq'], 'L0_attn_Wk': _L0_attn_in['Wk'], 'L0_attn_Wv': _L0_attn_in['Wv'], 'L0_attn_bv': _L0_attn_in['bv'], 'L0_attn_Wo': _L0_attn_in['Wo'], 'L0_attn_bo': _L0_attn_in['bo'], 'L0_ffn_shared_gate': _L0_ffn_in['shared_gate'], 'L0_ffn_shared_up': _L0_ffn_in['shared_up'], 'L0_ffn_shared_down': _L0_ffn_in['shared_down'], 'L0_ffn_gate_w': _L0_ffn_in['gate_w'], 'L0_ffn_up_w': _L0_ffn_in['up_w'], 'L0_ffn_down_w': _L0_ffn_in['down_w'], 'L0_ffn_router_w': _L0_ffn_in['router_w'], 'L0_ffn_routing_bias': _L0_ffn_in['routing_bias']}
    _x0 = _d['L0_attn_x']
    _d['L0_attn_x'] = jax.random.normal(jax.random.fold_in(jax.random.key(seed), 1), (32, 256, 128), dtype=_x0.dtype)
    del _x0
    return _d

def reference(L0_attn_x, L0_attn_Wq, L0_attn_bq, L0_attn_Wk, L0_attn_Wv, L0_attn_bv, L0_attn_Wo, L0_attn_bo, L0_ffn_shared_gate, L0_ffn_shared_up, L0_ffn_shared_down, L0_ffn_gate_w, L0_ffn_up_w, L0_ffn_down_w, L0_ffn_router_w, L0_ffn_routing_bias):

    def _L0_attn_ref(x, Wq, bq, Wk, Wv, bv, Wo, bo):
        import jax, jax.numpy as jnp
        import numpy as np
        N_HEAD = 16

        def _phi(x):
            return jax.nn.silu(x) + 1.0
        B, T, D = x.shape
        H = N_HEAD
        Dh = D // H
        scale = Dh ** (-0.25)
        q = x @ Wq.T + bq
        k = x @ Wk.T
        v = x @ Wv.T + bv
        q = q.reshape(B, T, H, Dh).transpose(0, 2, 1, 3) * scale
        k = k.reshape(B, T, H, Dh).transpose(0, 2, 1, 3) * scale
        v = v.reshape(B, T, H, Dh).transpose(0, 2, 1, 3)
        phi_q = _phi(q)
        phi_k = _phi(k)
        kv = jnp.einsum('bhtd,bhte->bhde', phi_k, v)
        out = jnp.einsum('bhtd,bhde->bhte', phi_q, kv)
        wv = out.transpose(0, 2, 1, 3).reshape(B, T, D)
        return wv @ Wo.T + bo

    def _L0_ffn_ref(x, shared_gate, shared_up, shared_down, gate_w, up_w, down_w, router_w, routing_bias):
        import jax, jax.numpy as jnp
        import numpy as np
        B, S, H = (2, 256, 128)
        E_ROUTED = 8
        TOP_K = 2
        I = 256
        b, s, h = x.shape
        shared = jnp.einsum('bsi,hi->bsh', jax.nn.silu(jnp.einsum('bsh,ih->bsi', x, shared_gate)) * jnp.einsum('bsh,ih->bsi', x, shared_up), shared_down)
        logits = jnp.einsum('bsh,eh->bse', x, router_w) + routing_bias
        probs = jax.nn.sigmoid(logits)
        scores, indices = jax.lax.top_k(probs, TOP_K)
        scores = scores / jnp.sum(scores, axis=-1, keepdims=True)
        t = b * s
        xf = x.reshape(t, h)
        idx = indices.reshape(t, TOP_K)
        sc = scores.reshape(t, TOP_K)
        w = jnp.zeros((t, E_ROUTED), dtype=x.dtype)
        w = w.at[jnp.arange(t)[:, None], idx].add(sc)
        g = jax.nn.silu(jnp.einsum('th,ehi->tei', xf, gate_w))
        u = jnp.einsum('th,ehi->tei', xf, up_w)
        combined = jnp.einsum('tei,eih,te->th', g * u, down_w, w)
        return shared + combined.reshape(b, s, h)
    x = L0_attn_x
    x = x + 0.5 * _L0_ffn_ref(_layernorm(x, axis=-1), L0_ffn_shared_gate, L0_ffn_shared_up, L0_ffn_shared_down, L0_ffn_gate_w, L0_ffn_up_w, L0_ffn_down_w, L0_ffn_router_w, L0_ffn_routing_bias)
    x = x + _L0_attn_ref(_layernorm(x, axis=-1), L0_attn_Wq, L0_attn_bq, L0_attn_Wk, L0_attn_Wv, L0_attn_bv, L0_attn_Wo, L0_attn_bo)
    x = x + 0.5 * _L0_ffn_ref(_layernorm(x, axis=-1), L0_ffn_shared_gate, L0_ffn_shared_up, L0_ffn_shared_down, L0_ffn_gate_w, L0_ffn_up_w, L0_ffn_down_w, L0_ffn_router_w, L0_ffn_routing_bias)
    return x

_drawn_inputs = setup_inputs


def setup_inputs(seed=0):
    import zlib

    import numpy as np

    out = dict(_drawn_inputs(seed))
    spreads = {'L0_ffn_routing_bias': (0.0, 0.8)}
    factors = {'L0_attn_bq': 22.833,
     'L0_attn_bo': 8.0,
     'L0_ffn_shared_gate': 8.0,
     'L0_ffn_shared_up': 8.0,
     'L0_ffn_shared_down': 8.0,
     'L0_ffn_gate_w': 8.0,
     'L0_ffn_up_w': 8.0,
     'L0_ffn_down_w': 8.0,
     'L0_ffn_router_w': 8.0}
    for name, (base, spread) in spreads.items():
        noise = np.random.default_rng([zlib.crc32(name.encode()), seed]).standard_normal(out[name].shape)
        drawn = base * np.exp(spread * noise) if base else spread * noise
        out[name] = jnp.asarray(drawn.astype(out[name].dtype))
    for name, factor in factors.items():
        out[name] = (out[name] * factor).astype(out[name].dtype)
    return out
```

```python
from contextlib import ExitStack

import concourse.bass as bass
from concourse import mybir

F32 = mybir.dt.float32
F32R = mybir.dt.float32r
ALU = mybir.AluOpType
ACT = mybir.ActivationFunctionType
AX_X = mybir.AxisListType.X

P = 128
SUB = 4
TT = P * SUB
EXPERTS = 9
ROUTED = EXPERTS - 1
INNER = 256
HALVES = INNER // P
CHUNKS = EXPERTS * HALVES
SHARED_CHUNKS = HALVES
WIDE = 2 * INNER + HALVES * P
HEADS = 16
HEAD = P // HEADS
EPS = 1e-5
SCALE = float(HEAD) ** -0.25
ROUTE_STEPS = 15

S_RING, HP_RING, H_RING, SPLIT_RING = 3, 2, 3, 4
LAG = 3


def wait_count(eng, sem, value):
    if isinstance(value, int) and value <= 0:
        return
    eng.wait_ge(sem, value)


def over_tiles(eng, tiles, body):
    body(0, 0)
    with eng.Fori(0, (tiles - 2) // 2) as pair:
        body(pair * 2 + 1, 1)
        body(pair * 2 + 2, 0)
    body(tiles - 1, 1)


def macaron(nc, x_in, w_experts, router_wT, routing_bias, w_attn, bq, bv, bo, out):
    tokens = x_in.shape[0]
    tiles = tokens // TT
    FFN1, ATTN, FFN2 = 0, tiles, 2 * tiles
    x_view = x_in.rearrange("(n b p j) d -> n p b (j d)", b=2, p=P, j=2)
    out_view = out.rearrange("(n b p j) d -> n p b (j d)", b=2, p=P, j=2)
    w_scratch = nc.dram_tensor("w_scratch", (ROUTED, SUB, P), F32, kind="Internal").ap()

    with ExitStack() as ctx:
        def sb(name, shape, dt=F32):
            return ctx.enter_context(nc.sbuf_tensor(name, shape, dt))

        def bank(name):
            return ctx.enter_context(nc.psum_tensor(name, [P, 512], F32))

        def sem(name):
            return ctx.enter_context(nc.semaphore(name))

        x = sb("x", [P, tiles, TT])
        w_raw = sb("w_raw", [P, 3, WIDE])
        w_hi = sb("w_hi", [P, EXPERTS, WIDE], F32R)
        w_lo = sb("w_lo", [P, EXPERTS, WIDE], F32R)
        attn_raw = sb("attn_raw", [P, 4 * P])
        attn_hi = sb("attn_hi", [P, 3 * P], F32R)
        attn_lo = sb("attn_lo", [P, 3 * P], F32R)
        wo = attn_raw[:, 3 * P:4 * P]
        router_raw = sb("router_raw", [P, ROUTED])
        router_hi = sb("router_hi", [P, ROUTED], F32R)
        router_lo = sb("router_lo", [P, ROUTED], F32R)
        bias_b = sb("bias_b", [P, ROUTED])
        bq_col = sb("bq_col", [P, 1])
        bq_scaled = sb("bq_scaled", [P, 1])
        bv_b = sb("bv_b", [P, P])
        bo_b = sb("bo_b", [P, P])
        ident = sb("ident", [P, P])
        earlier = sb("earlier", [P, SUB, ROUTED, ROUTED])
        head_mask = sb("head_mask", [P, P])
        neg_half = sb("neg_half", [P, SUB])
        eps = sb("eps", [P, SUB])
        ones = sb("ones", [P, TT])
        stats = sb("stats", [P, SUB, 6])
        mv = sb("mv", [P, SUB, 2])
        var_eps = sb("var_eps", [P, SUB])
        rstd = sb("rstd", [P, SUB])
        xn = sb("xn", [P, SUB, P])
        xT_hi = [sb(f"xT_hi{i}", [P, TT], F32R) for i in range(2)]
        xT_lo = [sb(f"xT_lo{i}", [P, TT], F32R) for i in range(2)]
        RW = SUB * ROUTED
        z = sb("z", [P, RW])
        z_square = sb("z_square", [P, RW])
        z_nudge = sb("z_nudge", [P, RW])
        z_safe = sb("z_safe", [P, RW])
        z_silu = sb("z_silu", [P, RW])
        z_recip = sb("z_recip", [P, RW])
        prob = sb("prob", [P, SUB, ROUTED])
        beaten = sb("beaten", [P, SUB, ROUTED, ROUTED])
        tied = sb("tied", [P, SUB, ROUTED, ROUTED])
        rank = sb("rank", [P, SUB, ROUTED])
        chosen = sb("chosen", [P, SUB, ROUTED])
        total = sb("total", [P, SUB])
        inv_total = sb("inv_total", [P, SUB])
        weight = sb("weight", [P, ROUTED, SUB])
        weightT = sb("weightT", [RW, P])
        weight_b = [sb(f"weight_b{i}", [P, ROUTED, TT]) for i in range(2)]
        silu_g = [sb(f"silu_g{i}", [P, TT]) for i in range(S_RING)]
        h_raw = [sb(f"h_raw{i}", [P, TT]) for i in range(HP_RING)]
        h = [sb(f"h{i}", [P, TT]) for i in range(H_RING)]
        h_hi = [sb(f"h_hi{i}", [P, TT], F32R) for i in range(SPLIT_RING)]
        h_lo = [sb(f"h_lo{i}", [P, TT], F32R) for i in range(SPLIT_RING)]
        yT = sb("yT", [P, TT])
        q_silu = sb("q_silu", [P, TT])
        k_silu = sb("k_silu", [P, SUB, P])
        phi_q = [sb(f"phi_q{i}", [P, TT]) for i in range(2)]
        phi_k = sb("phi_k", [P, SUB, P])
        v_sb = sb("v_sb", [P, SUB, P])
        kv_sb = sb("kv_sb", [P, 2, P])
        kvo_sb = sb("kvo_sb", [P, 2, P])

        g_bank = [bank("g_bank0"), bank("g_bank1")]
        u_bank = [bank("u_bank0"), bank("u_bank1")]
        y_bank = [bank("y_bank0"), bank("y_bank1")]
        tr_bank = bank("tr_bank")
        route_bank = bank("route_bank")
        q_bank, k_bank, v_bank, kv_bank = g_bank[0], u_bank[0], g_bank[1], u_bank[1]
        kvo_bank, att_bank = y_bank

        x_first, x_some, x_rest = sem("x_first"), sem("x_some"), sem("x_rest")
        router_loaded, attn_loaded = sem("router_loaded"), sem("attn_loaded")
        w_loaded = [sem(f"w_loaded{i}") for i in range(3)]
        ident_zero, consts_ready = sem("ident_zero"), sem("consts_ready")
        earlier_ready = sem("earlier_ready")
        split_hi, split_lo = sem("split_hi"), sem("split_lo")
        bq_ready = sem("bq_ready")
        stats_done, mv_done = sem("stats_done"), sem("mv_done")
        var_eps_done, rstd_done = sem("var_eps_done"), sem("rstd_done")
        xn_done, xT_psum = sem("xn_done"), sem("xT_psum")
        xT_hi_done, xT_lo_done = sem("xT_hi_done"), sem("xT_lo_done")
        logits_psum, route_step, z_silu_done = sem("logits_psum"), sem("route_step"), sem("z_silu_done")
        weightT_psum, weightT_done = sem("weightT_psum"), sem("weightT_done")
        weight_stored, weight_loaded = sem("weight_stored"), sem("weight_loaded")
        gu_psum, silu_done, h_raw_done = sem("gu_psum"), sem("silu_done"), sem("h_raw_done")
        h_done, h_hi_done, h_lo_done, down_done = sem("h_done"), sem("h_hi_done"), sem("h_lo_done"), sem("down_done")
        yT_done, y_psum, x_updated = sem("yT_done"), sem("y_psum"), sem("x_updated")
        q_psum, k_psum, v_psum = sem("q_psum"), sem("k_psum"), sem("v_psum")
        q_silu_done, k_silu_done, v_done = sem("q_silu_done"), sem("k_silu_done"), sem("v_done")
        phi_q_done, phi_k_done, x_biased = sem("phi_q_done"), sem("phi_k_done"), sem("x_biased")
        kv_psum, kv_done, kvo_psum, kvo_done = sem("kv_psum"), sem("kv_done"), sem("kvo_psum"), sem("kvo_done")
        att_psum, x_attended = sem("att_psum"), sem("x_attended")
        stored = sem("stored")

        SPLIT_ROUTER, SPLIT_ATTN = 1, EXPERTS + 2

        def split_expert(e):
            return e + 2

        def routed_chunks(f, k):
            return f * (CHUNKS - SHARED_CHUNKS) + (k - SHARED_CHUNKS + 1)

        def half(k):
            return k // HALVES, k % HALVES

        def w_gate(w, k):
            e, c = half(k)
            return w[:, e, c * P:(c + 1) * P]

        def w_up(w, k):
            e, c = half(k)
            return w[:, e, INNER + c * P:INNER + (c + 1) * P]

        def w_down(w, k):
            e, c = half(k)
            return w[:, e, 2 * INNER + c * P:2 * INNER + (c + 1) * P]

        def x_tile(t):
            return x[:, bass.ds(t, 1), :].rearrange("p a n -> p (a n)")

        def x_sub(t, j):
            return x[:, bass.ds(t, 1), j * P:(j + 1) * P].rearrange("p a n -> p (a n)")

        def spread_weights(sp, f, par):
            sp.wait_ge(weightT_done, f + 1)
            wait_count(sp, weight_loaded, f * 16)
            sp.dma_start(w_scratch.rearrange("e j p -> (e j) p"), weightT[:]).then_inc(weight_stored, 16)
            sp.wait_ge(weight_stored, (f + 1) * 16)
            if not (isinstance(f, int) and f < 2):
                sp.wait_ge(h_done, routed_chunks(f - 2, CHUNKS - 1))
            sp.dma_start(weight_b[par][:], w_scratch.rearrange("e j p -> e (j p)").partition_broadcast(P)
                         ).then_inc(weight_loaded, 16)

        block = ctx.enter_context(nc.Block())

        @block.sync
        def _(sp):
            sp.dma_start(x[:, 0, :].rearrange("p (b n) -> p b n", b=2), x_view[0]).then_inc(x_first, 16)
            sp.dma_start(router_raw[:], router_wT).then_inc(router_loaded, 16)
            sp.dma_start(bias_b[:], routing_bias.partition_broadcast(P)).then_inc(router_loaded, 16)
            for e in range(EXPERTS):
                if e >= 3:
                    sp.wait_ge(split_lo, split_expert(e - 3))
                sp.dma_start(w_raw[:, e % 3, :], w_experts[e]).then_inc(w_loaded[e % 3], 16)
                if e == 1:
                    for t in range(1, 4):
                        sp.dma_start(x[:, t, :].rearrange("p (b n) -> p b n", b=2), x_view[t]).then_inc(x_some, 16)
                if e == 2:
                    with sp.Fori(4, tiles) as t:
                        sp.dma_start(x[:, bass.ds(t, 1), :].rearrange("p a (b n) -> p (a b) n", b=2),
                                     x_view[bass.ds(t, 1)].rearrange("a p b n -> p (a b) n")).then_inc(x_rest, 16)
                    sp.dma_start(attn_raw[:], w_attn).then_inc(attn_loaded, 16)
                    sp.dma_start(bq_col[:], bq).then_inc(attn_loaded, 16)
                    sp.dma_start(bv_b[:], bv.partition_broadcast(P)).then_inc(attn_loaded, 16)
                    sp.dma_start(bo_b[:], bo.partition_broadcast(P)).then_inc(attn_loaded, 16)
                if e == 0:
                    spread_weights(sp, 0, 0)

            def ffn_tile(f0, last_next_routes):
                def body(t, par):
                    if not (isinstance(t, int) and t == tiles - 1):
                        spread_weights(sp, f0 + t + 1, 1 - par)
                    if f0:
                        if not (isinstance(t, int) and t == 0):
                            store_tile(t - 1)
                return body

            def store_tile(t):
                sp.wait_ge(x_updated, t + (tiles + 1))
                sp.dma_start(out_view[bass.ds(t, 1)].rearrange("a p b n -> p (a b) n"),
                             x[:, bass.ds(t, 1), :].rearrange("p a (b n) -> p (a b) n", b=2)).then_inc(stored, 16)

            over_tiles(sp, tiles, ffn_tile(0, False))
            spread_weights(sp, tiles, 0)
            over_tiles(sp, tiles, ffn_tile(tiles, False))
            store_tile(tiles - 1)
            sp.wait_ge(stored, 16 * tiles)

        @block.gpsimd
        def _(pool):
            pool.memset(ident[:], 0.0).then_inc(ident_zero, 1)
            pool.memset(head_mask[:], 1.0).then_inc(ident_zero, 1)
            pool.memset(neg_half[:], -0.5).then_inc(ident_zero, 1)
            pool.memset(eps[:], EPS).then_inc(ident_zero, 1)
            pool.memset(ones[:], 1.0).then_inc(ident_zero, 1)
            pool.wait_ge(ident_zero, 5)
            pool.affine_select(out=ident[:], in_=ident[:], compare_op=ALU.not_equal, fill=1.0, base=0,
                               pattern=[[-1, P]], channel_multiplier=1).then_inc(consts_ready, 1)
            mask = head_mask[:].rearrange("p (h d) -> p h d", d=HEAD)
            pool.affine_select(out=mask, in_=mask, compare_op=ALU.is_ge, fill=0.0, base=0,
                               pattern=[[-HEAD, HEADS], [0, HEAD]], channel_multiplier=1).then_inc(ident_zero, 1)
            pool.wait_ge(ident_zero, 6)
            pool.affine_select(out=mask, in_=mask, compare_op=ALU.is_ge, fill=0.0, base=HEAD - 1,
                               pattern=[[HEAD, HEADS], [0, HEAD]], channel_multiplier=-1).then_inc(consts_ready, 1)

            def norm_scale(step):
                pool.wait_ge(mv_done, step + 1)
                pool.tensor_tensor(var_eps[:], mv[:, :, 1], eps[:], ALU.add).then_inc(var_eps_done, 1)
                pool.wait_ge(var_eps_done, step + 1)
                pool.tensor_tensor(rstd[:], var_eps[:], neg_half[:], ALU.pow).then_inc(rstd_done, 1)

            def split_low(f, k):
                c = f * CHUNKS + k
                pool.wait_ge(h_hi_done, c + 1)
                pool.tensor_tensor(h_lo[k_slot(f, k, SPLIT_RING)][:], h[k_slot(f, k, H_RING)][:],
                                   h_hi[k_slot(f, k, SPLIT_RING)][:].bitcast(F32),
                                   ALU.subtract).then_inc(h_lo_done, 1)

            def ffn_tile(f0, step0):
                def body(t, par):
                    f = f0 + t
                    for k in range(CHUNKS):
                        split_low(Slot(f, par), k)
                        if k == 1 and not (f0 and isinstance(t, int) and t == tiles - 1):
                            norm_scale(step0 + t + 1)
                return body

            def attention_tile(t, par):
                norm_scale(ATTN + t + 1)
                pool.wait_ge(q_silu_done, t + 1)
                pool.tensor_tensor(phi_q[par][:], q_silu[:], ones[:], ALU.add).then_inc(phi_q_done, 1)
                pool.wait_ge(xn_done, ATTN + t + 1)
                if isinstance(t, int) and t == 0:
                    pool.wait_ge(attn_loaded, 64)
                xt = x[:, bass.ds(t, 1), :].rearrange("p a (s d) -> p (a s) d", s=SUB)
                pool.tensor_tensor(xt, xt, bo_b[:].unsqueeze(1).to_broadcast([P, SUB, P]),
                                   ALU.add).then_inc(x_biased, 1)

            norm_scale(0)
            over_tiles(pool, tiles, ffn_tile(0, FFN1))
            over_tiles(pool, tiles, attention_tile)
            over_tiles(pool, tiles, ffn_tile(tiles, FFN2))

        @block.scalar
        def _(act):
            def split_high(e):
                act.wait_ge(w_loaded[e % 3], 16 * (e // 3 + 1))
                act.activation(w_hi[:, e, :], w_raw[:, e % 3, :], ACT.Copy).then_inc(split_hi, 1)

            def xT_high(step, par):
                act.wait_ge(xT_psum, step + 1)
                act.activation(xT_hi[par][:], tr_bank[:], ACT.Copy).then_inc(xT_hi_done, 1)

            def h_high(f, k):
                c = f * CHUNKS + k
                if k < SHARED_CHUNKS:
                    act.wait_ge(h_raw_done, c + 1)
                else:
                    act.wait_ge(h_done, routed_chunks(f, k))
                wait_count(act, down_done, c - SPLIT_RING + 1)
                act.activation(h_hi[k_slot(f, k, SPLIT_RING)][:], h[k_slot(f, k, H_RING)][:],
                               ACT.Copy).then_inc(h_hi_done, 1)

            def y_out(f, par):
                act.wait_ge(down_done, f * CHUNKS + CHUNKS)
                act.activation(yT[:], y_bank[par][:], ACT.Copy).then_inc(yT_done, 1)

            def ffn_tile(f0, step0):
                def body(t, par):
                    f = Slot(f0 + t, par)
                    first = isinstance(t, int) and t == 0
                    last = isinstance(t, int) and t == tiles - 1
                    for k in range(CHUNKS):
                        c = f * CHUNKS + k
                        act.wait_ge(gu_psum, c + 1)
                        wait_count(act, h_raw_done, c - S_RING + 1)
                        act.activation(silu_g[k_slot(f, k, S_RING)][:], g_bank[k % 2][:],
                                       ACT.Silu).then_inc(silu_done, 1)
                        if k == 0:
                            if not first:
                                h_high(f.before(), CHUNKS - 1)
                        else:
                            h_high(f, k - 1)
                        if f0 == 0 and first:
                            if k % 2 == 0 and k // 2 + 1 < EXPERTS:
                                split_high(k // 2 + 1)
                            if k == CHUNKS - 2:
                                act.wait_ge(attn_loaded, 64)
                                act.activation(attn_hi[:], attn_raw[:, 0:3 * P], ACT.Copy).then_inc(split_hi, 1)
                        if k == 3 and not first:
                            y_out((f0 + t) - 1, 1 - par)
                        if k == 4 and not (f0 and last):
                            xT_high(step0 + t + 1, 1 - par)
                        if k == 7 and not last:
                            route_silu(f0 + t + 1)
                return body

            def route_silu(f):
                act.wait_ge(route_step, f * ROUTE_STEPS + 4)
                act.activation(z_silu[:], z_safe[:], ACT.Silu).then_inc(z_silu_done, 1)

            def attention_tile(t, par):
                act.wait_ge(k_psum, t + 1)
                wait_count(act, phi_k_done, t)
                act.activation(k_silu[:].rearrange("p s d -> p (s d)"), k_bank[:], ACT.Silu,
                               scale=SCALE).then_inc(k_silu_done, 1)
                act.wait_ge(q_psum, t + 1)
                wait_count(act, phi_q_done, t)
                if isinstance(t, int) and t == 0:
                    act.wait_ge(bq_ready, 1)
                act.activation(q_silu[:], q_bank[:], ACT.Silu, bias=bq_scaled[:, 0:1],
                               scale=SCALE).then_inc(q_silu_done, 1)
                xT_high(ATTN + t + 1, 1 - par)
                act.wait_ge(kvo_psum, t + 1)
                wait_count(act, att_psum, t)
                act.activation(kvo_sb[:].rearrange("p b d -> p (b d)"), kvo_bank[:, 0:2 * P],
                               ACT.Copy).then_inc(kvo_done, 1)

            act.wait_ge(router_loaded, 32)
            act.activation(router_hi[:], router_raw[:], ACT.Copy).then_inc(split_hi, 1)
            split_high(0)
            xT_high(0, 0)
            route_silu(0)
            over_tiles(act, tiles, ffn_tile(0, FFN1))
            h_high(Slot(tiles - 1, 1), CHUNKS - 1)
            y_out(tiles - 1, 1)
            over_tiles(act, tiles, attention_tile)
            route_silu(tiles)
            over_tiles(act, tiles, ffn_tile(tiles, FFN2))
            h_high(Slot(2 * tiles - 1, 1), CHUNKS - 1)
            y_out(2 * tiles - 1, 1)

        @block.tensor
        def _(pe):
            def three(bank_ap, w_parts, x_parts, start, stop):
                pe.matmul(bank_ap, w_parts[0], x_parts[0], start=start, stop=False)
                pe.matmul(bank_ap, w_parts[0], x_parts[1], start=False, stop=False)
                return pe.matmul(bank_ap, w_parts[1], x_parts[0], start=False, stop=stop)

            def transpose_x(step):
                pe.wait_ge(xn_done, step + 1)
                wait_count(pe, xT_lo_done, step)
                for j in range(SUB):
                    last = pe.transpose(tr_bank[:, j * P:(j + 1) * P], xn[:, j, :], ident[:])
                last.then_inc(xT_psum, 1)

            def router(f, step, par):
                pe.wait_ge(xT_lo_done, step + 1)
                wait_count(pe, weightT_done, f)
                for j in range(SUB):
                    s = slice(j * P, (j + 1) * P)
                    last = three(route_bank[:, j * ROUTED:(j + 1) * ROUTED],
                                 (xT_hi[par][:, s], xT_lo[par][:, s]), (router_hi[:], router_lo[:]), True, True)
                last.then_inc(logits_psum, 1)

            def transpose_weights(f):
                pe.wait_ge(route_step, (f + 1) * ROUTE_STEPS)
                pe.transpose(route_bank[0:RW, P:2 * P], weight[:].rearrange("p e j -> p (e j)"),
                             ident[:]).then_inc(weightT_psum, 1)

            def down(f, k, par):
                pe.wait_ge(h_lo_done, f * CHUNKS + k + 1)
                s = k_slot(f, k, SPLIT_RING)
                three(y_bank[par][:], (w_down(w_hi, k), w_down(w_lo, k)), (h_hi[s][:], h_lo[s][:]),
                      k == 0, k == CHUNKS - 1).then_inc(down_done, 1)

            def transpose_y(f, step):
                pe.wait_ge(yT_done, f + 1)
                pe.wait_ge(xT_lo_done, step + 1)
                for j in range(SUB):
                    last = pe.transpose(tr_bank[:, j * P:(j + 1) * P], yT[:, j * P:(j + 1) * P], ident[:])
                last.then_inc(y_psum, 1)

            def ffn_tile(f0, step0):
                def body(t, par):
                    f = Slot(f0 + t, par)
                    first = isinstance(t, int) and t == 0
                    last = isinstance(t, int) and t == tiles - 1
                    if first and f0:
                        pe.wait_ge(x_attended, tiles)
                    for k in range(CHUNKS):
                        c = f * CHUNKS + k
                        if k == 0:
                            pe.wait_ge(xT_lo_done, step0 + t + 1)
                        if f0 == 0 and first and k % HALVES == 0:
                            pe.wait_ge(split_lo, split_expert(k // HALVES))
                        wait_count(pe, h_raw_done, c - 1)
                        xs = (xT_hi[par][:], xT_lo[par][:])
                        three(g_bank[k % 2][:], (w_gate(w_hi, k), w_gate(w_lo, k)), xs, True, True)
                        three(u_bank[k % 2][:], (w_up(w_hi, k), w_up(w_lo, k)), xs, True, True).then_inc(gu_psum, 1)
                        if k >= LAG:
                            down(f, k - LAG, par)
                        elif not first:
                            down(f.before(), CHUNKS - LAG + k, 1 - par)
                        if k == 3 and not (f0 and last):
                            transpose_x(step0 + t + 1)
                        if k == 5 and not last:
                            router(f0 + t + 1, step0 + t + 1 + 0, 1 - par)
                        if k == 6 and not first:
                            transpose_y((f0 + t) - 1, step0 + t + (0 if (f0 and last) else 1))
                        if k == 12 and not last:
                            transpose_weights(f0 + t + 1)
                return body

            def drain(f, step):
                for k in range(CHUNKS - LAG, CHUNKS):
                    down(Slot(f, 1), k, 1)
                transpose_y(f, step)

            def attention_tile(t, par):
                if isinstance(t, int) and t == 0:
                    pe.wait_ge(x_updated, tiles)
                    pe.wait_ge(split_lo, SPLIT_ATTN)
                pe.wait_ge(xT_lo_done, ATTN + t + 1)
                wait_count(pe, k_silu_done, t)
                wait_count(pe, v_done, t)
                for n, (kv_out, done) in enumerate(((k_bank, k_psum), (v_bank, v_psum))):
                    w = slice((1 + n) * P, (2 + n) * P)
                    for j in range(SUB):
                        s = slice(j * P, (j + 1) * P)
                        last = three(kv_out[:, s], (xT_hi[par][:, s], xT_lo[par][:, s]),
                                     (attn_hi[:, w], attn_lo[:, w]), True, True)
                    last.then_inc(done, 1)
                wait_count(pe, q_silu_done, t)
                three(q_bank[:], (attn_hi[:, 0:P], attn_lo[:, 0:P]), (xT_hi[par][:], xT_lo[par][:]),
                      True, True).then_inc(q_psum, 1)
                if not (isinstance(t, int) and t == 0):
                    attend(t - 1, 1 - par)
                transpose_x(ATTN + t + 1)
                pe.wait_ge(phi_k_done, t + 1)
                pe.wait_ge(v_done, t + 1)
                wait_count(pe, kv_done, t)
                for b in range(2):
                    for j in range(2):
                        last = pe.matmul(kv_bank[:, b * P:(b + 1) * P], v_sb[:, 2 * b + j, :],
                                         phi_k[:, 2 * b + j, :], start=(j == 0), stop=(j == 1))
                last.then_inc(kv_psum, 1)
                pe.wait_ge(kv_done, t + 1)
                wait_count(pe, kvo_done, t)
                for b in range(2):
                    last = pe.matmul(kvo_bank[:, b * P:(b + 1) * P], kv_sb[:, b, :], wo, start=True, stop=True)
                last.then_inc(kvo_psum, 1)

            def attend(t, par):
                pe.wait_ge(kvo_done, t + 1)
                pe.wait_ge(phi_q_done, t + 1)
                for j in range(SUB):
                    last = pe.matmul(att_bank[:, j * P:(j + 1) * P], phi_q[par][:, j * P:(j + 1) * P],
                                     kvo_sb[:, j // 2, :], start=True, stop=True)
                last.then_inc(att_psum, 1)

            pe.wait_ge(consts_ready, 1)
            transpose_x(0)
            pe.wait_ge(split_lo, SPLIT_ROUTER)
            router(0, 0, 0)
            transpose_weights(0)
            over_tiles(pe, tiles, ffn_tile(0, FFN1))
            drain(tiles - 1, ATTN)
            over_tiles(pe, tiles, attention_tile)
            attend(tiles - 1, 1)
            router(tiles, FFN2, 0)
            transpose_weights(tiles)
            over_tiles(pe, tiles, ffn_tile(tiles, FFN2))
            drain(2 * tiles - 1, FFN2 + tiles - 1)

        @block.vector
        def _(dve):
            def split_low(e):
                dve.wait_ge(split_hi, split_expert(e))
                dve.tensor_tensor(w_lo[:, e, :], w_raw[:, e % 3, :], w_hi[:, e, :].bitcast(F32),
                                  ALU.subtract).then_inc(split_lo, 1)

            def norm_stats(t):
                for j in range(SUB):
                    last = dve.bn_stats(stats[:, j, :], x_sub(t, j))
                last.then_inc(stats_done, 1)

            def norm_mean():
                for j in range(SUB):
                    last = dve.bn_aggr(mv[:, j, :], stats[:, j, :])
                last.then_inc(mv_done, 1)

            def normalise(t, step):
                dve.wait_ge(rstd_done, step + 1)
                dve.wait_ge(mv_done, step + 1)
                wait_count(dve, xT_psum, step)
                for j in range(SUB):
                    last = dve.tensor_scalar(xn[:, j, :], x_sub(t, j), mv[:, j, 0:1], rstd[:, j:j + 1],
                                             ALU.subtract, ALU.mult)
                last.then_inc(xn_done, 1)

            def xT_low(step, par):
                dve.wait_ge(xT_hi_done, step + 1)
                dve.tensor_tensor(xT_lo[par][:], tr_bank[:], xT_hi[par][:].bitcast(F32),
                                  ALU.subtract).then_inc(xT_lo_done, 1)

            def route(f, n):
                r = f * ROUTE_STEPS
                pf = prob[:].unsqueeze(2).to_broadcast([P, SUB, ROUTED, ROUTED])
                pe_ = prob[:].unsqueeze(3).to_broadcast([P, SUB, ROUTED, ROUTED])
                if n == 0:
                    dve.wait_ge(logits_psum, f + 1)
                    dve.tensor_tensor(z[:].rearrange("p (j e) -> p j e", e=ROUTED),
                                      route_bank[:, 0:RW].rearrange("p (j e) -> p j e", e=ROUTED),
                                      bias_b[:].unsqueeze(1).to_broadcast([P, SUB, ROUTED]),
                                      ALU.add).then_inc(route_step, 1)
                    dve.wait_ge(route_step, r + 1)
                    dve.tensor_tensor(z_square[:], z[:], z[:], ALU.mult).then_inc(route_step, 1)
                    dve.wait_ge(route_step, r + 2)
                    dve.tensor_scalar(z_nudge[:], z_square[:], 1e-36, 2e-18, ALU.is_lt, ALU.mult).then_inc(route_step, 1)
                    dve.wait_ge(route_step, r + 3)
                    dve.tensor_tensor(z_safe[:], z[:], z_nudge[:], ALU.add).then_inc(route_step, 1)
                if n == 1:
                    dve.wait_ge(route_step, r + 4)
                    dve.reciprocal(z_recip[:], z_safe[:]).then_inc(route_step, 1)
                    dve.wait_ge(route_step, r + 5)
                    dve.wait_ge(z_silu_done, f + 1)
                    dve.tensor_tensor(prob[:].rearrange("p j e -> p (j e)"), z_silu[:], z_recip[:],
                                      ALU.mult).then_inc(route_step, 1)
                    dve.wait_ge(route_step, r + 6)
                    dve.tensor_tensor(beaten[:], pf, pe_, ALU.is_gt).then_inc(route_step, 1)
                if n == 2:
                    dve.tensor_tensor(tied[:], pf, pe_, ALU.is_equal).then_inc(route_step, 1)
                    dve.wait_ge(route_step, r + 8)
                    dve.tensor_tensor(tied[:], tied[:], earlier[:], ALU.mult).then_inc(route_step, 1)
                    dve.wait_ge(route_step, r + 9)
                    dve.tensor_tensor(beaten[:], beaten[:], tied[:], ALU.add).then_inc(route_step, 1)
                if n == 3:
                    dve.wait_ge(route_step, r + 10)
                    dve.tensor_reduce(rank[:], beaten[:], AX_X, ALU.add).then_inc(route_step, 1)
                    dve.wait_ge(route_step, r + 11)
                    dve.scalar_tensor_tensor(out=chosen[:], in0=rank[:], scalar=1.5, in1=prob[:], op0=ALU.is_lt,
                                             op1=ALU.mult).then_inc(route_step, 1)
                if n == 4:
                    dve.wait_ge(route_step, r + 12)
                    dve.tensor_reduce(total[:], chosen[:], AX_X, ALU.add).then_inc(route_step, 1)
                    dve.wait_ge(route_step, r + 13)
                    dve.reciprocal(inv_total[:], total[:]).then_inc(route_step, 1)
                    dve.wait_ge(route_step, r + 14)
                    wait_count(dve, weightT_psum, f)
                    dve.tensor_tensor(weight[:].rearrange("p e j -> p j e"), chosen[:],
                                      inv_total[:].unsqueeze(2).to_broadcast([P, SUB, ROUTED]),
                                      ALU.mult).then_inc(route_step, 1)

            def weights_out(f):
                dve.wait_ge(weightT_psum, f + 1)
                wait_count(dve, weight_stored, f * 16)
                dve.tensor_copy(weightT[:], route_bank[0:RW, P:2 * P]).then_inc(weightT_done, 1)

            def gate_up(f, k):
                c = f * CHUNKS + k
                dve.wait_ge(silu_done, c + 1)
                if k < SHARED_CHUNKS:
                    wait_count(dve, h_lo_done, c - H_RING + 1)
                    dst = h[k_slot(f, k, H_RING)]
                else:
                    dst = h_raw[k % HP_RING]
                dve.tensor_tensor(dst[:], silu_g[k_slot(f, k, S_RING)][:], u_bank[k % 2][:],
                                  ALU.mult).then_inc(h_raw_done, 1)

            def weigh(f, k, par):
                c = f * CHUNKS + k
                dve.wait_ge(h_raw_done, c + 1)
                if k == SHARED_CHUNKS:
                    dve.wait_ge(weight_loaded, (f.index + 1) * 16)
                wait_count(dve, h_lo_done, c - H_RING + 1)
                dve.tensor_tensor(h[k_slot(f, k, H_RING)][:], h_raw[k % HP_RING][:],
                                  weight_b[par][:, k // HALVES - 1, :], ALU.mult).then_inc(h_done, 1)

            def add_y(t, f):
                dve.wait_ge(y_psum, f + 1)
                dve.scalar_tensor_tensor(out=x_tile(t), in0=tr_bank[:], scalar=0.5, in1=x_tile(t), op0=ALU.mult,
                                         op1=ALU.add).then_inc(x_updated, 1)

            def ffn_tile(f0, step0):
                def body(t, par):
                    f = Slot(f0 + t, par)
                    first = isinstance(t, int) and t == 0
                    last = isinstance(t, int) and t == tiles - 1
                    prep = not (f0 and last)
                    nt = 0 if last else t + 1
                    ns = step0 + t + 1
                    for k in range(CHUNKS):
                        if prep and k == 1:
                            dve.wait_ge(stats_done, ns + 1)
                        gate_up(f, k)
                        if k == 0:
                            if not first:
                                weigh(f.before(), CHUNKS - 1, 1 - par)
                        elif k > SHARED_CHUNKS:
                            weigh(f, k - 1, par)
                        if f0 == 0 and first:
                            if k % 2 == 0 and k // 2 + 1 < EXPERTS:
                                split_low(k // 2 + 1)
                            if k == CHUNKS - 2:
                                dve.wait_ge(split_hi, SPLIT_ATTN)
                                dve.tensor_tensor(attn_lo[:], attn_raw[:, 0:3 * P], attn_hi[:].bitcast(F32),
                                                  ALU.subtract).then_inc(split_lo, 1)
                                dve.tensor_scalar(bq_scaled[:], bq_col[:], SCALE, None, ALU.mult).then_inc(bq_ready, 1)
                        if prep and k == 0:
                            if f0 == 0 and first:
                                dve.wait_ge(x_some, 48)
                            norm_stats(nt)
                        if prep and k == 1:
                            norm_mean()
                        if prep and k == 2:
                            if f0 == 0 and first:
                                dve.wait_ge(x_rest, 16 * (tiles - 4))
                            normalise(nt, ns)
                        if prep and k == 4:
                            xT_low(ns, 1 - par)
                        if k >= 6 and k < 11 and not last:
                            route(f0 + t + 1, k - 6)
                        if k == 7 and not first:
                            add_y(t - 1, (f0 + t) - 1)
                        if k == 13 and not last:
                            weights_out(f0 + t + 1)
                return body

            def drain(f):
                weigh(Slot(f, 1), CHUNKS - 1, 1)
                add_y(tiles - 1, f)

            def attention_tile(t, par):
                last = isinstance(t, int) and t == tiles - 1
                nt = 0 if last else t + 1
                ns = ATTN + t + 1
                norm_stats(nt)
                dve.wait_ge(stats_done, ns + 1)
                dve.wait_ge(k_silu_done, t + 1)
                wait_count(dve, kv_psum, t)
                dve.tensor_scalar(phi_k[:], k_silu[:], 1.0, None, ALU.add).then_inc(phi_k_done, 1)
                norm_mean()
                dve.wait_ge(v_psum, t + 1)
                dve.tensor_tensor(v_sb[:], v_bank[:].rearrange("p (s d) -> p s d", s=SUB),
                                  bv_b[:].unsqueeze(1).to_broadcast([P, SUB, P]), ALU.add).then_inc(v_done, 1)
                normalise(nt, ns)
                xT_low(ns, 1 - par)
                if not (isinstance(t, int) and t == 0):
                    add_attention(t - 1)
                dve.wait_ge(kv_psum, t + 1)
                wait_count(dve, kvo_psum, t)
                dve.tensor_tensor(kv_sb[:], kv_bank[:, 0:2 * P].rearrange("p (b d) -> p b d", b=2),
                                  head_mask[:].unsqueeze(1).to_broadcast([P, 2, P]), ALU.mult).then_inc(kv_done, 1)

            def add_attention(t):
                dve.wait_ge(att_psum, t + 1)
                dve.wait_ge(x_biased, t + 1)
                dve.tensor_tensor(x_tile(t), att_bank[:], x_tile(t), ALU.add).then_inc(x_attended, 1)

            dve.memset(earlier[:], 0.0).then_inc(earlier_ready, 1)
            dve.wait_ge(earlier_ready, 1)
            for e in range(1, ROUTED):
                last_set = dve.memset(earlier[:, :, e, 0:e], 1.0)
            last_set.then_inc(earlier_ready, 1)
            dve.wait_ge(x_first, 16)
            norm_stats(0)
            dve.wait_ge(stats_done, 1)
            norm_mean()
            normalise(0, 0)
            dve.wait_ge(split_hi, SPLIT_ROUTER)
            dve.tensor_tensor(router_lo[:], router_raw[:], router_hi[:].bitcast(F32),
                              ALU.subtract).then_inc(split_lo, 1)
            split_low(0)
            xT_low(0, 0)
            dve.wait_ge(earlier_ready, 2)
            for n in range(5):
                route(0, n)
            weights_out(0)
            over_tiles(dve, tiles, ffn_tile(0, FFN1))
            drain(tiles - 1)
            dve.wait_ge(consts_ready, 2)
            over_tiles(dve, tiles, attention_tile)
            add_attention(tiles - 1)
            for n in range(5):
                route(tiles, n)
            weights_out(tiles)
            over_tiles(dve, tiles, ffn_tile(tiles, FFN2))
            drain(2 * tiles - 1)


class Slot:

    def __init__(self, index, parity):
        self.index, self.parity = index, parity

    def __mul__(self, n):
        return self.index * n

    def before(self):
        return Slot(self.index - 1, 1 - self.parity)


def k_slot(f, k, ring):
    assert (2 * CHUNKS) % ring == 0
    return (f.parity * CHUNKS + k) % ring


_OUT = ((32, 256, 128), "float32")


def kernel(**inputs):
    import numpy as np
    import concourse.bacc as bacc
    from concourse.bass_utils import run_bass_kernel_spmd

    a = {k: np.asarray(v) for k, v in inputs.items()}
    gate = np.concatenate([a["L0_ffn_shared_gate"].T[None], a["L0_ffn_gate_w"]])
    up = np.concatenate([a["L0_ffn_shared_up"].T[None], a["L0_ffn_up_w"]])
    down = np.concatenate([a["L0_ffn_shared_down"].T[None], a["L0_ffn_down_w"]])
    arrays = {
        "x_in": a["L0_attn_x"].reshape(-1, P),
        "w_experts": np.concatenate([gate, up, down[:, :P], down[:, P:]], axis=2),
        "router_wT": a["L0_ffn_router_w"].T,
        "routing_bias": a["L0_ffn_routing_bias"],
        "w_attn": np.concatenate([a["L0_attn_" + n].T for n in ("Wq", "Wk", "Wv", "Wo")], axis=1),
        "bq": a["L0_attn_bq"].reshape(P, 1),
        "bv": a["L0_attn_bv"],
        "bo": a["L0_attn_bo"],
    }
    arrays = {k: np.ascontiguousarray(v) for k, v in arrays.items()}
    nc = bacc.Bacc("TRN2", target_bir_lowering=False, num_devices=1)
    args = [nc.dram_tensor(k, v.shape, mybir.dt.from_np(v.dtype), kind="ExternalInput").ap() for k, v in arrays.items()]
    out = nc.dram_tensor("out", (a["L0_attn_x"].size // P, P), F32, kind="ExternalOutput").ap()
    macaron(nc, *args, out)
    result = run_bass_kernel_spmd(nc, [arrays], core_ids=[0])
    return result.results[0]["out"].reshape(_OUT[0])
```

```python
from contextlib import ExitStack

import concourse.bass as bass
from concourse import mybir

F32 = mybir.dt.float32
F32R = mybir.dt.float32r
ALU = mybir.AluOpType
ACT = mybir.ActivationFunctionType
AX_X = mybir.AxisListType.X

P = 128
SUB = 4
TT = P * SUB
EXPERTS = 9
ROUTED = EXPERTS - 1
INNER = 256
HALVES = INNER // P
CHUNKS = EXPERTS * HALVES
SHARED_CHUNKS = HALVES
WIDE = 2 * INNER + HALVES * P
HEADS = 16
HEAD = P // HEADS
EPS = 1e-5
SCALE = float(HEAD) ** -0.25
ROUTE_AT = {8: (0, 1, 2), 9: (3, 4), 11: (5, 6, 7), 12: (8, 9, 10), 13: (11, 12, 13, 14)}
ROUTE_STEPS = 15

S_RING, HP_RING, H_RING, SPLIT_RING = 3, 2, 4, 6
HIGH_LAG = 2
LAG = 5


def wait_count(eng, sem, value):
    if isinstance(value, int) and value <= 0:
        return
    eng.wait_ge(sem, value)


def over_tiles(eng, tiles, body):
    body(0, 0)
    with eng.Fori(0, (tiles - 2) // 2) as pair:
        body(pair * 2 + 1, 1)
        body(pair * 2 + 2, 0)
    body(tiles - 1, 1)


def macaron(nc, x_in, w_experts, router_wT, routing_bias, w_attn, bq, bv, bo, out):
    tokens = x_in.shape[0]
    tiles = tokens // TT
    FFN1, ATTN, FFN2 = 0, tiles, 2 * tiles
    x_view = x_in.rearrange("(n b p j) d -> n p b (j d)", b=2, p=P, j=2)
    out_view = out.rearrange("(n b p j) d -> n p b (j d)", b=2, p=P, j=2)
    w_scratch = nc.dram_tensor("w_scratch", (ROUTED, SUB, P), F32, kind="Internal").ap()

    with ExitStack() as ctx:
        def sb(name, shape, dt=F32):
            return ctx.enter_context(nc.sbuf_tensor(name, shape, dt))

        def bank(name):
            return ctx.enter_context(nc.psum_tensor(name, [P, 512], F32))

        def sem(name):
            return ctx.enter_context(nc.semaphore(name))

        x = sb("x", [P, tiles, TT])
        w_raw = sb("w_raw", [P, 3, WIDE])
        w_hi = sb("w_hi", [P, EXPERTS, WIDE], F32R)
        w_lo = sb("w_lo", [P, EXPERTS, WIDE], F32R)
        attn_raw = sb("attn_raw", [P, 4 * P])
        attn_hi = sb("attn_hi", [P, 3 * P], F32R)
        attn_lo = sb("attn_lo", [P, 3 * P], F32R)
        wo = attn_raw[:, 3 * P:4 * P]
        router_raw = sb("router_raw", [P, ROUTED])
        router_hi = sb("router_hi", [P, ROUTED], F32R)
        router_lo = sb("router_lo", [P, ROUTED], F32R)
        bias_b = sb("bias_b", [P, ROUTED])
        bq_col = sb("bq_col", [P, 1])
        bq_scaled = sb("bq_scaled", [P, 1])
        bv_b = sb("bv_b", [P, P])
        bo_b = sb("bo_b", [P, P])
        ident = sb("ident", [P, P])
        earlier = sb("earlier", [P, SUB, ROUTED, ROUTED])
        head_mask = sb("head_mask", [P, P])
        neg_half = sb("neg_half", [P, SUB])
        eps = sb("eps", [P, SUB])
        ones = sb("ones", [P, TT])
        stats = sb("stats", [P, SUB, 6])
        mv = sb("mv", [P, SUB, 2])
        var_eps = sb("var_eps", [P, SUB])
        rstd = sb("rstd", [P, SUB])
        xn = sb("xn", [P, SUB, P])
        xT_hi = [sb(f"xT_hi{i}", [P, TT], F32R) for i in range(2)]
        xT_lo = [sb(f"xT_lo{i}", [P, TT], F32R) for i in range(2)]
        RW = SUB * ROUTED
        z = sb("z", [P, RW])
        z_square = sb("z_square", [P, RW])
        z_nudge = sb("z_nudge", [P, RW])
        z_safe = sb("z_safe", [P, RW])
        z_silu = sb("z_silu", [P, RW])
        z_recip = sb("z_recip", [P, RW])
        prob = sb("prob", [P, SUB, ROUTED])
        beaten = sb("beaten", [P, SUB, ROUTED, ROUTED])
        tied = sb("tied", [P, SUB, ROUTED, ROUTED])
        rank = sb("rank", [P, SUB, ROUTED])
        chosen = sb("chosen", [P, SUB, ROUTED])
        total = sb("total", [P, SUB])
        inv_total = sb("inv_total", [P, SUB])
        weight = sb("weight", [P, ROUTED, SUB])
        weightT = sb("weightT", [RW, P])
        weight_b = [sb(f"weight_b{i}", [P, ROUTED, TT]) for i in range(2)]
        silu_g = [sb(f"silu_g{i}", [P, TT]) for i in range(S_RING)]
        h_raw = [sb(f"h_raw{i}", [P, TT]) for i in range(HP_RING)]
        h = [sb(f"h{i}", [P, TT]) for i in range(H_RING)]
        h_hi = [sb(f"h_hi{i}", [P, TT], F32R) for i in range(SPLIT_RING)]
        h_lo = [sb(f"h_lo{i}", [P, TT], F32R) for i in range(SPLIT_RING)]
        yT = sb("yT", [P, TT])
        q_silu = silu_g[0][:]
        k_silu = silu_g[1][:].rearrange("p (s d) -> p s d", s=SUB)
        phi_q = [sb(f"phi_q{i}", [P, TT]) for i in range(2)]
        phi_k = sb("phi_k", [P, SUB, P])
        v_sb = h_raw[0][:].rearrange("p (s d) -> p s d", s=SUB)
        kv_sb = sb("kv_sb", [P, 2, P])
        kvo_sb = sb("kvo_sb", [P, 2, P])

        g_bank = [bank("g_bank0"), bank("g_bank1")]
        u_bank = [bank("u_bank0"), bank("u_bank1")]
        y_bank = [bank("y_bank0"), bank("y_bank1")]
        tr_bank = bank("tr_bank")
        route_bank = bank("route_bank")
        q_bank, k_bank, v_bank, kv_bank = g_bank[0], u_bank[0], g_bank[1], u_bank[1]
        kvo_bank, att_bank = y_bank

        x_first, x_some, x_rest = sem("x_first"), sem("x_some"), sem("x_rest")
        router_loaded, attn_loaded = sem("router_loaded"), sem("attn_loaded")
        w_loaded = [sem(f"w_loaded{i}") for i in range(3)]
        ident_zero, consts_ready = sem("ident_zero"), sem("consts_ready")
        earlier_ready = sem("earlier_ready")
        split_hi, split_lo = sem("split_hi"), sem("split_lo")
        bq_ready = sem("bq_ready")
        stats_done, mv_done = sem("stats_done"), sem("mv_done")
        var_eps_done, rstd_done = sem("var_eps_done"), sem("rstd_done")
        xn_done, xT_psum = sem("xn_done"), sem("xT_psum")
        xT_hi_done, xT_lo_done = sem("xT_hi_done"), sem("xT_lo_done")
        logits_psum, route_step, z_silu_done = sem("logits_psum"), sem("route_step"), sem("z_silu_done")
        weightT_psum, weightT_done = sem("weightT_psum"), sem("weightT_done")
        weight_stored, weight_loaded = sem("weight_stored"), sem("weight_loaded")
        gu_psum, silu_done, h_raw_done = sem("gu_psum"), sem("silu_done"), sem("h_raw_done")
        h_done, h_hi_done, h_lo_done, down_done = sem("h_done"), sem("h_hi_done"), sem("h_lo_done"), sem("down_done")
        yT_done, y_psum, x_updated = sem("yT_done"), sem("y_psum"), sem("x_updated")
        q_psum, k_psum, v_psum = sem("q_psum"), sem("k_psum"), sem("v_psum")
        q_silu_done, k_silu_done, v_done = sem("q_silu_done"), sem("k_silu_done"), sem("v_done")
        phi_q_done, phi_k_done, x_biased = sem("phi_q_done"), sem("phi_k_done"), sem("x_biased")
        kv_psum, kv_done, kvo_psum, kvo_done = sem("kv_psum"), sem("kv_done"), sem("kvo_psum"), sem("kvo_done")
        att_psum, x_attended = sem("att_psum"), sem("x_attended")
        stored = sem("stored")

        SPLIT_ROUTER, SPLIT_ATTN = 1, EXPERTS + 2

        def split_expert(e):
            return e + 2

        def routed_chunks(f, k):
            return f * (CHUNKS - SHARED_CHUNKS) + (k - SHARED_CHUNKS + 1)

        def half(k):
            return k // HALVES, k % HALVES

        def w_gate(w, k):
            e, c = half(k)
            return w[:, e, c * P:(c + 1) * P]

        def w_up(w, k):
            e, c = half(k)
            return w[:, e, INNER + c * P:INNER + (c + 1) * P]

        def w_down(w, k):
            e, c = half(k)
            return w[:, e, 2 * INNER + c * P:2 * INNER + (c + 1) * P]

        def x_tile(t):
            return x[:, bass.ds(t, 1), :].rearrange("p a n -> p (a n)")

        def x_sub(t, j):
            return x[:, bass.ds(t, 1), j * P:(j + 1) * P].rearrange("p a n -> p (a n)")

        def spread_weights(sp, f, par):
            sp.wait_ge(weightT_done, f + 1)
            wait_count(sp, weight_loaded, f * 16)
            sp.dma_start(w_scratch.rearrange("e j p -> (e j) p"), weightT[:]).then_inc(weight_stored, 16)
            sp.wait_ge(weight_stored, (f + 1) * 16)
            if not (isinstance(f, int) and f < 2):
                sp.wait_ge(h_done, routed_chunks(f - 2, CHUNKS - 1))
            sp.dma_start(weight_b[par][:], w_scratch.rearrange("e j p -> e (j p)").partition_broadcast(P)
                         ).then_inc(weight_loaded, 16)

        block = ctx.enter_context(nc.Block())

        @block.sync
        def _(sp):
            sp.dma_start(x[:, 0, :].rearrange("p (b n) -> p b n", b=2), x_view[0]).then_inc(x_first, 16)
            sp.dma_start(router_raw[:], router_wT).then_inc(router_loaded, 16)
            sp.dma_start(bias_b[:], routing_bias.partition_broadcast(P)).then_inc(router_loaded, 16)
            for e in range(EXPERTS):
                if e >= 3:
                    sp.wait_ge(split_lo, split_expert(e - 3))
                sp.dma_start(w_raw[:, e % 3, :], w_experts[e]).then_inc(w_loaded[e % 3], 16)
                if e == 1:
                    for t in range(1, 4):
                        sp.dma_start(x[:, t, :].rearrange("p (b n) -> p b n", b=2), x_view[t]).then_inc(x_some, 16)
                if e == 2:
                    with sp.Fori(4, tiles) as t:
                        sp.dma_start(x[:, bass.ds(t, 1), :].rearrange("p a (b n) -> p (a b) n", b=2),
                                     x_view[bass.ds(t, 1)].rearrange("a p b n -> p (a b) n")).then_inc(x_rest, 16)
                    sp.dma_start(attn_raw[:], w_attn).then_inc(attn_loaded, 16)
                    sp.dma_start(bq_col[:], bq).then_inc(attn_loaded, 16)
                    sp.dma_start(bv_b[:], bv.partition_broadcast(P)).then_inc(attn_loaded, 16)
                    sp.dma_start(bo_b[:], bo.partition_broadcast(P)).then_inc(attn_loaded, 16)
                if e == 0:
                    spread_weights(sp, 0, 0)

            def ffn_tile(f0, last_next_routes):
                def body(t, par):
                    if not (isinstance(t, int) and t == tiles - 1):
                        spread_weights(sp, f0 + t + 1, 1 - par)
                    if f0:
                        if not (isinstance(t, int) and t == 0):
                            store_tile(t - 1)
                return body

            def store_tile(t):
                sp.wait_ge(x_updated, t + (tiles + 1))
                sp.dma_start(out_view[bass.ds(t, 1)].rearrange("a p b n -> p (a b) n"),
                             x[:, bass.ds(t, 1), :].rearrange("p a (b n) -> p (a b) n", b=2)).then_inc(stored, 16)

            over_tiles(sp, tiles, ffn_tile(0, False))
            spread_weights(sp, tiles, 0)
            over_tiles(sp, tiles, ffn_tile(tiles, False))
            store_tile(tiles - 1)
            sp.wait_ge(stored, 16 * tiles)

        @block.gpsimd
        def _(pool):
            pool.memset(ident[:], 0.0).then_inc(ident_zero, 1)
            pool.memset(head_mask[:], 1.0).then_inc(ident_zero, 1)
            pool.memset(neg_half[:], -0.5).then_inc(ident_zero, 1)
            pool.memset(eps[:], EPS).then_inc(ident_zero, 1)
            pool.memset(ones[:], 1.0).then_inc(ident_zero, 1)
            pool.wait_ge(ident_zero, 5)
            pool.affine_select(out=ident[:], in_=ident[:], compare_op=ALU.not_equal, fill=1.0, base=0,
                               pattern=[[-1, P]], channel_multiplier=1).then_inc(consts_ready, 1)
            mask = head_mask[:].rearrange("p (h d) -> p h d", d=HEAD)
            pool.affine_select(out=mask, in_=mask, compare_op=ALU.is_ge, fill=0.0, base=0,
                               pattern=[[-HEAD, HEADS], [0, HEAD]], channel_multiplier=1).then_inc(ident_zero, 1)
            pool.wait_ge(ident_zero, 6)
            pool.affine_select(out=mask, in_=mask, compare_op=ALU.is_ge, fill=0.0, base=HEAD - 1,
                               pattern=[[HEAD, HEADS], [0, HEAD]], channel_multiplier=-1).then_inc(consts_ready, 1)

            def norm_scale(step):
                pool.wait_ge(mv_done, step + 1)
                pool.tensor_tensor(var_eps[:], mv[:, :, 1], eps[:], ALU.add).then_inc(var_eps_done, 1)
                pool.wait_ge(var_eps_done, step + 1)
                pool.tensor_tensor(rstd[:], var_eps[:], neg_half[:], ALU.pow).then_inc(rstd_done, 1)

            def split_low(f, k):
                c = f * CHUNKS + k
                pool.wait_ge(h_hi_done, c + 1)
                pool.tensor_tensor(h_lo[k_slot(f, k, SPLIT_RING)][:], h[k_slot(f, k, H_RING)][:],
                                   h_hi[k_slot(f, k, SPLIT_RING)][:].bitcast(F32),
                                   ALU.subtract).then_inc(h_lo_done, 1)

            def ffn_tile(f0, step0):
                def body(t, par):
                    f = f0 + t
                    for k in range(CHUNKS):
                        if k == 0 and not (f0 and isinstance(t, int) and t == tiles - 1):
                            norm_scale(step0 + t + 1)
                        split_low(Slot(f, par), k)
                return body

            def attention_tile(t, par):
                norm_scale(ATTN + t + 1)
                pool.wait_ge(q_silu_done, t + 1)
                pool.tensor_tensor(phi_q[par][:], q_silu, ones[:], ALU.add).then_inc(phi_q_done, 1)
                pool.wait_ge(xn_done, ATTN + t + 1)
                if isinstance(t, int) and t == 0:
                    pool.wait_ge(attn_loaded, 64)
                xt = x[:, bass.ds(t, 1), :].rearrange("p a (s d) -> p (a s) d", s=SUB)
                pool.tensor_tensor(xt, xt, bo_b[:].unsqueeze(1).to_broadcast([P, SUB, P]),
                                   ALU.add).then_inc(x_biased, 1)

            norm_scale(0)
            over_tiles(pool, tiles, ffn_tile(0, FFN1))
            over_tiles(pool, tiles, attention_tile)
            over_tiles(pool, tiles, ffn_tile(tiles, FFN2))

        @block.scalar
        def _(act):
            def split_high(e):
                act.wait_ge(w_loaded[e % 3], 16 * (e // 3 + 1))
                act.activation(w_hi[:, e, :], w_raw[:, e % 3, :], ACT.Copy).then_inc(split_hi, 1)

            def xT_high(step, par):
                act.wait_ge(xT_psum, step + 1)
                act.activation(xT_hi[par][:], tr_bank[:], ACT.Copy).then_inc(xT_hi_done, 1)

            def h_high(f, k):
                c = f * CHUNKS + k
                if k < SHARED_CHUNKS:
                    act.wait_ge(h_raw_done, c + 1)
                else:
                    act.wait_ge(h_done, routed_chunks(f, k))
                wait_count(act, down_done, c - SPLIT_RING + 1)
                act.activation(h_hi[k_slot(f, k, SPLIT_RING)][:], h[k_slot(f, k, H_RING)][:],
                               ACT.Copy).then_inc(h_hi_done, 1)

            def y_out(f, par):
                act.wait_ge(down_done, f * CHUNKS + CHUNKS)
                act.activation(yT[:], y_bank[par][:], ACT.Copy).then_inc(yT_done, 1)

            def ffn_tile(f0, step0):
                def body(t, par):
                    f = Slot(f0 + t, par)
                    first = isinstance(t, int) and t == 0
                    last = isinstance(t, int) and t == tiles - 1
                    for k in range(CHUNKS):
                        c = f * CHUNKS + k
                        act.wait_ge(gu_psum, c + 1)
                        wait_count(act, h_raw_done, c - S_RING + 1)
                        act.activation(silu_g[k_slot(f, k, S_RING)][:], g_bank[k % 2][:],
                                       ACT.Silu).then_inc(silu_done, 1)
                        if k >= HIGH_LAG:
                            h_high(f, k - HIGH_LAG)
                        elif not first:
                            h_high(f.before(), CHUNKS + k - HIGH_LAG)
                        if f0 == 0 and first:
                            if k % 2 == 0 and k // 2 + 1 < EXPERTS:
                                split_high(k // 2 + 1)
                            if k == CHUNKS - 2:
                                act.wait_ge(attn_loaded, 64)
                                act.activation(attn_hi[:], attn_raw[:, 0:3 * P], ACT.Copy).then_inc(split_hi, 1)
                        if k == 5 and not first:
                            y_out((f0 + t) - 1, 1 - par)
                        if k == 6 and not (f0 and last):
                            xT_high(step0 + t + 1, 1 - par)
                        if k == 9 and not last:
                            route_silu(f0 + t + 1)
                return body

            def route_silu(f):
                act.wait_ge(route_step, f * ROUTE_STEPS + 4)
                act.activation(z_silu[:], z_safe[:], ACT.Silu).then_inc(z_silu_done, 1)

            def attention_tile(t, par):
                act.wait_ge(k_psum, t + 1)
                wait_count(act, phi_k_done, t)
                act.activation(silu_g[1][:], k_bank[:], ACT.Silu,
                               scale=SCALE).then_inc(k_silu_done, 1)
                act.wait_ge(q_psum, t + 1)
                wait_count(act, phi_q_done, t)
                if isinstance(t, int) and t == 0:
                    act.wait_ge(bq_ready, 1)
                act.activation(q_silu, q_bank[:], ACT.Silu, bias=bq_scaled[:, 0:1],
                               scale=SCALE).then_inc(q_silu_done, 1)
                xT_high(ATTN + t + 1, 1 - par)
                act.wait_ge(kvo_psum, t + 1)
                wait_count(act, att_psum, t)
                act.activation(kvo_sb[:].rearrange("p b d -> p (b d)"), kvo_bank[:, 0:2 * P],
                               ACT.Copy).then_inc(kvo_done, 1)

            act.wait_ge(router_loaded, 32)
            act.activation(router_hi[:], router_raw[:], ACT.Copy).then_inc(split_hi, 1)
            split_high(0)
            xT_high(0, 0)
            route_silu(0)
            over_tiles(act, tiles, ffn_tile(0, FFN1))
            for k in range(CHUNKS - HIGH_LAG, CHUNKS):
                h_high(Slot(tiles - 1, 1), k)
            y_out(tiles - 1, 1)
            over_tiles(act, tiles, attention_tile)
            route_silu(tiles)
            over_tiles(act, tiles, ffn_tile(tiles, FFN2))
            for k in range(CHUNKS - HIGH_LAG, CHUNKS):
                h_high(Slot(2 * tiles - 1, 1), k)
            y_out(2 * tiles - 1, 1)

        @block.tensor
        def _(pe):
            def three(bank_ap, w_parts, x_parts, start, stop):
                pe.matmul(bank_ap, w_parts[0], x_parts[0], start=start, stop=False)
                pe.matmul(bank_ap, w_parts[0], x_parts[1], start=False, stop=False)
                return pe.matmul(bank_ap, w_parts[1], x_parts[0], start=False, stop=stop)

            def transpose_x(step):
                pe.wait_ge(xn_done, step + 1)
                wait_count(pe, xT_lo_done, step)
                for j in range(SUB):
                    last = pe.transpose(tr_bank[:, j * P:(j + 1) * P], xn[:, j, :], ident[:])
                last.then_inc(xT_psum, 1)

            def router(f, step, par):
                pe.wait_ge(xT_lo_done, step + 1)
                wait_count(pe, weightT_done, f)
                for j in range(SUB):
                    s = slice(j * P, (j + 1) * P)
                    last = three(route_bank[:, j * ROUTED:(j + 1) * ROUTED],
                                 (xT_hi[par][:, s], xT_lo[par][:, s]), (router_hi[:], router_lo[:]), True, True)
                last.then_inc(logits_psum, 1)

            def transpose_weights(f):
                pe.wait_ge(route_step, (f + 1) * ROUTE_STEPS)
                pe.transpose(route_bank[0:RW, P:2 * P], weight[:].rearrange("p e j -> p (e j)"),
                             ident[:]).then_inc(weightT_psum, 1)

            def down(f, k, par):
                pe.wait_ge(h_lo_done, f * CHUNKS + k + 1)
                s = k_slot(f, k, SPLIT_RING)
                three(y_bank[par][:], (w_down(w_hi, k), w_down(w_lo, k)), (h_hi[s][:], h_lo[s][:]),
                      k == 0, k == CHUNKS - 1).then_inc(down_done, 1)

            def transpose_y(f, step):
                pe.wait_ge(yT_done, f + 1)
                pe.wait_ge(xT_lo_done, step + 1)
                for j in range(SUB):
                    last = pe.transpose(tr_bank[:, j * P:(j + 1) * P], yT[:, j * P:(j + 1) * P], ident[:])
                last.then_inc(y_psum, 1)

            def ffn_tile(f0, step0):
                def body(t, par):
                    f = Slot(f0 + t, par)
                    first = isinstance(t, int) and t == 0
                    last = isinstance(t, int) and t == tiles - 1
                    if first and f0:
                        pe.wait_ge(x_attended, tiles)
                    for k in range(CHUNKS):
                        c = f * CHUNKS + k
                        if k == 0:
                            pe.wait_ge(xT_lo_done, step0 + t + 1)
                        if f0 == 0 and first and k % HALVES == 0:
                            pe.wait_ge(split_lo, split_expert(k // HALVES))
                        wait_count(pe, h_raw_done, c - 1)
                        xs = (xT_hi[par][:], xT_lo[par][:])
                        three(g_bank[k % 2][:], (w_gate(w_hi, k), w_gate(w_lo, k)), xs, True, True)
                        three(u_bank[k % 2][:], (w_up(w_hi, k), w_up(w_lo, k)), xs, True, True).then_inc(gu_psum, 1)
                        if k >= LAG:
                            down(f, k - LAG, par)
                        elif not first:
                            down(f.before(), CHUNKS - LAG + k, 1 - par)
                        if k == 5 and not (f0 and last):
                            transpose_x(step0 + t + 1)
                        if k == 7 and not last:
                            router(f0 + t + 1, step0 + t + 1 + 0, 1 - par)
                        if k == 8 and not first:
                            transpose_y((f0 + t) - 1, step0 + t + (0 if (f0 and last) else 1))
                        if k == 14 and not last:
                            transpose_weights(f0 + t + 1)
                return body

            def drain(f, step):
                for k in range(CHUNKS - LAG, CHUNKS):
                    down(Slot(f, 1), k, 1)
                transpose_y(f, step)

            def attention_tile(t, par):
                if isinstance(t, int) and t == 0:
                    pe.wait_ge(x_updated, tiles)
                    pe.wait_ge(split_lo, SPLIT_ATTN)
                pe.wait_ge(xT_lo_done, ATTN + t + 1)
                wait_count(pe, k_silu_done, t)
                wait_count(pe, v_done, t)
                for n, (kv_out, done) in enumerate(((k_bank, k_psum), (v_bank, v_psum))):
                    w = slice((1 + n) * P, (2 + n) * P)
                    for j in range(SUB):
                        s = slice(j * P, (j + 1) * P)
                        last = three(kv_out[:, s], (xT_hi[par][:, s], xT_lo[par][:, s]),
                                     (attn_hi[:, w], attn_lo[:, w]), True, True)
                    last.then_inc(done, 1)
                wait_count(pe, q_silu_done, t)
                three(q_bank[:], (attn_hi[:, 0:P], attn_lo[:, 0:P]), (xT_hi[par][:], xT_lo[par][:]),
                      True, True).then_inc(q_psum, 1)
                if not (isinstance(t, int) and t == 0):
                    attend(t - 1, 1 - par)
                transpose_x(ATTN + t + 1)
                pe.wait_ge(phi_k_done, t + 1)
                pe.wait_ge(v_done, t + 1)
                wait_count(pe, kv_done, t)
                for b in range(2):
                    for j in range(2):
                        last = pe.matmul(kv_bank[:, b * P:(b + 1) * P], v_sb[:, 2 * b + j, :],
                                         phi_k[:, 2 * b + j, :], start=(j == 0), stop=(j == 1))
                last.then_inc(kv_psum, 1)
                pe.wait_ge(kv_done, t + 1)
                wait_count(pe, kvo_done, t)
                for b in range(2):
                    last = pe.matmul(kvo_bank[:, b * P:(b + 1) * P], kv_sb[:, b, :], wo, start=True, stop=True)
                last.then_inc(kvo_psum, 1)

            def attend(t, par):
                pe.wait_ge(kvo_done, t + 1)
                pe.wait_ge(phi_q_done, t + 1)
                for j in range(SUB):
                    last = pe.matmul(att_bank[:, j * P:(j + 1) * P], phi_q[par][:, j * P:(j + 1) * P],
                                     kvo_sb[:, j // 2, :], start=True, stop=True)
                last.then_inc(att_psum, 1)

            pe.wait_ge(consts_ready, 1)
            transpose_x(0)
            pe.wait_ge(split_lo, SPLIT_ROUTER)
            router(0, 0, 0)
            transpose_weights(0)
            over_tiles(pe, tiles, ffn_tile(0, FFN1))
            drain(tiles - 1, ATTN)
            over_tiles(pe, tiles, attention_tile)
            attend(tiles - 1, 1)
            router(tiles, FFN2, 0)
            transpose_weights(tiles)
            over_tiles(pe, tiles, ffn_tile(tiles, FFN2))
            drain(2 * tiles - 1, FFN2 + tiles - 1)

        @block.vector
        def _(dve):
            def split_low(e):
                dve.wait_ge(split_hi, split_expert(e))
                dve.tensor_tensor(w_lo[:, e, :], w_raw[:, e % 3, :], w_hi[:, e, :].bitcast(F32),
                                  ALU.subtract).then_inc(split_lo, 1)

            def norm_stats(t):
                for j in range(SUB):
                    last = dve.bn_stats(stats[:, j, :], x_sub(t, j))
                last.then_inc(stats_done, 1)

            def norm_mean():
                for j in range(SUB):
                    last = dve.bn_aggr(mv[:, j, :], stats[:, j, :])
                last.then_inc(mv_done, 1)

            def normalise(t, step):
                dve.wait_ge(rstd_done, step + 1)
                dve.wait_ge(mv_done, step + 1)
                wait_count(dve, xT_psum, step)
                for j in range(SUB):
                    last = dve.tensor_scalar(xn[:, j, :], x_sub(t, j), mv[:, j, 0:1], rstd[:, j:j + 1],
                                             ALU.subtract, ALU.mult)
                last.then_inc(xn_done, 1)

            def xT_low(step, par):
                dve.wait_ge(xT_hi_done, step + 1)
                dve.tensor_tensor(xT_lo[par][:], tr_bank[:], xT_hi[par][:].bitcast(F32),
                                  ALU.subtract).then_inc(xT_lo_done, 1)

            def route(f, n):
                r = f * ROUTE_STEPS
                other = prob[:].unsqueeze(2).to_broadcast([P, SUB, ROUTED, ROUTED])
                own = prob[:].unsqueeze(3).to_broadcast([P, SUB, ROUTED, ROUTED])
                if n > 0:
                    dve.wait_ge(route_step, r + n)
                if n == 0:
                    dve.wait_ge(logits_psum, f + 1)
                    op = dve.tensor_tensor(z[:].rearrange("p (j e) -> p j e", e=ROUTED),
                                           route_bank[:, 0:RW].rearrange("p (j e) -> p j e", e=ROUTED),
                                           bias_b[:].unsqueeze(1).to_broadcast([P, SUB, ROUTED]), ALU.add)
                if n == 1:
                    op = dve.tensor_tensor(z_square[:], z[:], z[:], ALU.mult)
                if n == 2:
                    op = dve.tensor_scalar(z_nudge[:], z_square[:], 1e-36, 2e-18, ALU.is_lt, ALU.mult)
                if n == 3:
                    op = dve.tensor_tensor(z_safe[:], z[:], z_nudge[:], ALU.add)
                if n == 4:
                    op = dve.reciprocal(z_recip[:], z_safe[:])
                if n == 5:
                    dve.wait_ge(z_silu_done, f + 1)
                    op = dve.tensor_tensor(prob[:].rearrange("p j e -> p (j e)"), z_silu[:], z_recip[:], ALU.mult)
                if n == 6:
                    op = dve.tensor_tensor(beaten[:], other, own, ALU.is_gt)
                if n == 7:
                    op = dve.tensor_tensor(tied[:], other, own, ALU.is_equal)
                if n == 8:
                    op = dve.tensor_tensor(tied[:], tied[:], earlier[:], ALU.mult)
                if n == 9:
                    op = dve.tensor_tensor(beaten[:], beaten[:], tied[:], ALU.add)
                if n == 10:
                    op = dve.tensor_reduce(rank[:], beaten[:], AX_X, ALU.add)
                if n == 11:
                    op = dve.scalar_tensor_tensor(out=chosen[:], in0=rank[:], scalar=1.5, in1=prob[:],
                                                  op0=ALU.is_lt, op1=ALU.mult)
                if n == 12:
                    op = dve.tensor_reduce(total[:], chosen[:], AX_X, ALU.add)
                if n == 13:
                    op = dve.reciprocal(inv_total[:], total[:])
                if n == 14:
                    wait_count(dve, weightT_psum, f)
                    op = dve.tensor_tensor(weight[:].rearrange("p e j -> p j e"), chosen[:],
                                           inv_total[:].unsqueeze(2).to_broadcast([P, SUB, ROUTED]), ALU.mult)
                op.then_inc(route_step, 1)

            def weights_out(f):
                dve.wait_ge(weightT_psum, f + 1)
                wait_count(dve, weight_stored, f * 16)
                dve.tensor_copy(weightT[:], route_bank[0:RW, P:2 * P]).then_inc(weightT_done, 1)

            def gate_up(f, k):
                c = f * CHUNKS + k
                dve.wait_ge(silu_done, c + 1)
                if k < SHARED_CHUNKS:
                    wait_count(dve, h_lo_done, c - H_RING + 1)
                    dst = h[k_slot(f, k, H_RING)]
                else:
                    before = routed_chunks(f, k - HP_RING) if k >= SHARED_CHUNKS + HP_RING else f * (
                        CHUNKS - SHARED_CHUNKS) + (k - SHARED_CHUNKS - HP_RING + 1)
                    wait_count(dve, h_done, before)
                    dst = h_raw[k % HP_RING]
                dve.tensor_tensor(dst[:], silu_g[k_slot(f, k, S_RING)][:], u_bank[k % 2][:],
                                  ALU.mult).then_inc(h_raw_done, 1)

            def weigh(f, k, par):
                c = f * CHUNKS + k
                dve.wait_ge(h_raw_done, c + 1)
                if k == SHARED_CHUNKS:
                    dve.wait_ge(weight_loaded, (f.index + 1) * 16)
                wait_count(dve, h_lo_done, c - H_RING + 1)
                dve.tensor_tensor(h[k_slot(f, k, H_RING)][:], h_raw[k % HP_RING][:],
                                  weight_b[par][:, k // HALVES - 1, :], ALU.mult).then_inc(h_done, 1)

            def add_y(t, f):
                dve.wait_ge(y_psum, f + 1)
                dve.scalar_tensor_tensor(out=x_tile(t), in0=tr_bank[:], scalar=0.5, in1=x_tile(t), op0=ALU.mult,
                                         op1=ALU.add).then_inc(x_updated, 1)

            def ffn_tile(f0, step0):
                def body(t, par):
                    f = Slot(f0 + t, par)
                    first = isinstance(t, int) and t == 0
                    last = isinstance(t, int) and t == tiles - 1
                    prep = not (f0 and last)
                    nt = 0 if last else t + 1
                    ns = step0 + t + 1
                    for k in range(CHUNKS):
                        if prep and k == 1:
                            dve.wait_ge(stats_done, ns + 1)
                        gate_up(f, k)
                        if k == 0:
                            if not first:
                                weigh(f.before(), CHUNKS - 1, 1 - par)
                        elif k > SHARED_CHUNKS:
                            weigh(f, k - 1, par)
                        if f0 == 0 and first:
                            if k % 2 == 0 and k // 2 + 1 < EXPERTS:
                                split_low(k // 2 + 1)
                            if k == CHUNKS - 2:
                                dve.wait_ge(split_hi, SPLIT_ATTN)
                                dve.tensor_tensor(attn_lo[:], attn_raw[:, 0:3 * P], attn_hi[:].bitcast(F32),
                                                  ALU.subtract).then_inc(split_lo, 1)
                                dve.tensor_scalar(bq_scaled[:], bq_col[:], SCALE, None, ALU.mult).then_inc(bq_ready, 1)
                        if prep and k == 0:
                            if f0 == 0 and first:
                                dve.wait_ge(x_some, 48)
                            norm_stats(nt)
                        if prep and k == 1:
                            norm_mean()
                        if prep and k == 3:
                            if f0 == 0 and first:
                                dve.wait_ge(x_rest, 16 * (tiles - 4))
                            normalise(nt, ns)
                        if prep and k == 6:
                            xT_low(ns, 1 - par)
                        if not last and k in ROUTE_AT:
                            for n in ROUTE_AT[k]:
                                route(f0 + t + 1, n)
                        if k == 9 and not first:
                            add_y(t - 1, (f0 + t) - 1)
                        if k == 15 and not last:
                            weights_out(f0 + t + 1)
                return body

            def drain(f):
                weigh(Slot(f, 1), CHUNKS - 1, 1)
                add_y(tiles - 1, f)

            def attention_tile(t, par):
                last = isinstance(t, int) and t == tiles - 1
                nt = 0 if last else t + 1
                ns = ATTN + t + 1
                norm_stats(nt)
                dve.wait_ge(stats_done, ns + 1)
                dve.wait_ge(k_silu_done, t + 1)
                wait_count(dve, kv_psum, t)
                dve.tensor_scalar(phi_k[:], k_silu, 1.0, None, ALU.add).then_inc(phi_k_done, 1)
                norm_mean()
                dve.wait_ge(v_psum, t + 1)
                dve.tensor_tensor(v_sb, v_bank[:].rearrange("p (s d) -> p s d", s=SUB),
                                  bv_b[:].unsqueeze(1).to_broadcast([P, SUB, P]), ALU.add).then_inc(v_done, 1)
                normalise(nt, ns)
                xT_low(ns, 1 - par)
                if not (isinstance(t, int) and t == 0):
                    add_attention(t - 1)
                dve.wait_ge(kv_psum, t + 1)
                wait_count(dve, kvo_psum, t)
                dve.tensor_tensor(kv_sb[:], kv_bank[:, 0:2 * P].rearrange("p (b d) -> p b d", b=2),
                                  head_mask[:].unsqueeze(1).to_broadcast([P, 2, P]), ALU.mult).then_inc(kv_done, 1)

            def add_attention(t):
                dve.wait_ge(att_psum, t + 1)
                dve.wait_ge(x_biased, t + 1)
                dve.tensor_tensor(x_tile(t), att_bank[:], x_tile(t), ALU.add).then_inc(x_attended, 1)

            dve.memset(earlier[:], 0.0).then_inc(earlier_ready, 1)
            dve.wait_ge(earlier_ready, 1)
            for e in range(1, ROUTED):
                last_set = dve.memset(earlier[:, :, e, 0:e], 1.0)
            last_set.then_inc(earlier_ready, 1)
            dve.wait_ge(x_first, 16)
            norm_stats(0)
            dve.wait_ge(stats_done, 1)
            norm_mean()
            normalise(0, 0)
            dve.wait_ge(split_hi, SPLIT_ROUTER)
            dve.tensor_tensor(router_lo[:], router_raw[:], router_hi[:].bitcast(F32),
                              ALU.subtract).then_inc(split_lo, 1)
            split_low(0)
            xT_low(0, 0)
            dve.wait_ge(earlier_ready, 2)
            for n in range(ROUTE_STEPS):
                route(0, n)
            weights_out(0)
            over_tiles(dve, tiles, ffn_tile(0, FFN1))
            drain(tiles - 1)
            dve.wait_ge(consts_ready, 2)
            over_tiles(dve, tiles, attention_tile)
            add_attention(tiles - 1)
            for n in range(ROUTE_STEPS):
                route(tiles, n)
            weights_out(tiles)
            over_tiles(dve, tiles, ffn_tile(tiles, FFN2))
            drain(2 * tiles - 1)


class Slot:

    def __init__(self, index, parity):
        self.index, self.parity = index, parity

    def __mul__(self, n):
        return self.index * n

    def before(self):
        return Slot(self.index - 1, 1 - self.parity)


def k_slot(f, k, ring):
    assert (2 * CHUNKS) % ring == 0
    return (f.parity * CHUNKS + k) % ring


_OUT = ((32, 256, 128), "float32")


def kernel(**inputs):
    import numpy as np
    import concourse.bacc as bacc
    from concourse.bass_utils import run_bass_kernel_spmd

    a = {k: np.asarray(v) for k, v in inputs.items()}
    gate = np.concatenate([a["L0_ffn_shared_gate"].T[None], a["L0_ffn_gate_w"]])
    up = np.concatenate([a["L0_ffn_shared_up"].T[None], a["L0_ffn_up_w"]])
    down = np.concatenate([a["L0_ffn_shared_down"].T[None], a["L0_ffn_down_w"]])
    arrays = {
        "x_in": a["L0_attn_x"].reshape(-1, P),
        "w_experts": np.concatenate([gate, up, down[:, :P], down[:, P:]], axis=2),
        "router_wT": a["L0_ffn_router_w"].T,
        "routing_bias": a["L0_ffn_routing_bias"],
        "w_attn": np.concatenate([a["L0_attn_" + n].T for n in ("Wq", "Wk", "Wv", "Wo")], axis=1),
        "bq": a["L0_attn_bq"].reshape(P, 1),
        "bv": a["L0_attn_bv"],
        "bo": a["L0_attn_bo"],
    }
    arrays = {k: np.ascontiguousarray(v) for k, v in arrays.items()}
    nc = bacc.Bacc("TRN2", target_bir_lowering=False, num_devices=1)
    args = [nc.dram_tensor(k, v.shape, mybir.dt.from_np(v.dtype), kind="ExternalInput").ap() for k, v in arrays.items()]
    out = nc.dram_tensor("out", (a["L0_attn_x"].size // P, P), F32, kind="ExternalOutput").ap()
    macaron(nc, *args, out)
    result = run_bass_kernel_spmd(nc, [arrays], core_ids=[0])
    return result.results[0]["out"].reshape(_OUT[0])
```

```python
from contextlib import ExitStack

import concourse.bass as bass
from concourse import mybir

F32 = mybir.dt.float32
F32R = mybir.dt.float32r
BF16 = mybir.dt.bfloat16
I32 = mybir.dt.int32
ALU = mybir.AluOpType
ACT = mybir.ActivationFunctionType
AX_X = mybir.AxisListType.X

P = 128
SUB = 4
TT = P * SUB
EXPERTS = 9
ROUTED = EXPERTS - 1
PICKS = 2
INNER = 256
HALVES = INNER // P
WIDE = 2 * INNER + HALVES * P
HEADS = 16
HEAD = P // HEADS
EPS = 1e-5
SCALE = float(HEAD) ** -0.25
Y_RING = 4
ROW = P + 1
ROUTE_STEPS = 25
LATE = 13
MASK_STEP, PSUM_READ_STEP = 13, 21
LOGITS = slice(0, 2 * SUB * ROUTED)
RANKS = slice(2 * SUB * ROUTED, 2 * SUB * ROUTED + (SUB + 1) * ROUTED)


class Ix:

    def __init__(self, t, par=None, half=None):
        self.t = t
        self.par = t % 2 if par is None else par
        self.half = t // 2 if half is None else half

    splits = False

    def at(self, d):
        return Ix(self.t + d, (self.par + d) % 2, self.half + (self.par + d) // 2)

    def is_(self, *values):
        return isinstance(self.t, int) and self.t in values


def wait_count(eng, sem, value):
    if isinstance(value, int) and value <= 0:
        return
    eng.wait_ge(sem, value)


def pairs(eng, lo, hi, body):
    with eng.Fori(lo, hi) as p:
        body(Ix(p * 2 + 1, 1, p))
        body(Ix(p * 2 + 2, 0, p + 1))


def over_tiles(eng, tiles, f, body):
    if f:
        return over(eng, tiles, body)

    def splitting(i):
        i.splits = True
        body(i)

    body(Ix(0))
    splitting(Ix(1))
    splitting(Ix(2))
    pairs(eng, 1, ROUTED // 2, splitting)
    pairs(eng, ROUTED // 2, (tiles - 3) // 2, body)
    for t in range(tiles - 3, tiles):
        body(Ix(t))


def over(eng, count, body, first_pair=1):
    last_pair = (count - 3) // 2
    for t in range(2 * first_pair + 1):
        body(Ix(t))
    pairs(eng, first_pair, last_pair, body)
    for t in range(2 * last_pair + 1, count):
        body(Ix(t))


def macaron(nc, x_in, w_experts, router_wT, routing_bias, w_attn, bq, bv, bo, out):
    tokens = x_in.shape[0]
    tiles = tokens // TT
    slots = PICKS * tiles + ROUTED - 1
    region = tokens + TT
    nobody = PICKS * tokens
    FFN1, ATTN, FFN2 = 0, tiles, 2 * tiles
    per_ffn = tiles + slots
    M_ATTN = per_ffn
    SLOTS_OF = (slots - slots // 2, slots // 2)
    TILES_OF = tiles // 2

    x_view = x_in.rearrange("(n b p j) d -> n p b (j d)", b=2, p=P, j=2)
    out_view = out.rearrange("(n b p j) d -> n p b (j d)", b=2, p=P, j=2)
    x_rows = nc.dram_tensor("x_rows", (ROUTED * region + TT, ROW), F32, kind="Internal").ap()
    y_rows = nc.dram_tensor("y_rows", (nobody + 2 * TT, P), F32, kind="Internal").ap()
    y_view = y_rows[0:nobody].rearrange("(n b p j w) d -> n p b (j w d)", b=2, p=P, j=2, w=PICKS)

    with ExitStack() as ctx:
        def sb(name, shape, dt=F32):
            return ctx.enter_context(nc.sbuf_tensor(name, shape, dt))

        def bank(name):
            return ctx.enter_context(nc.psum_tensor(name, [P, 512], F32))

        def sem(name):
            return ctx.enter_context(nc.semaphore(name))

        def two(name, shape, dt=F32):
            return [sb(f"{name}{i}", shape, dt) for i in range(2)]

        x = sb("x", [P, tiles, TT])
        w_raw = two("w_raw", [P, WIDE])
        w_gu = sb("w_gu", [P, EXPERTS, 2, 2 * INNER], F32R)
        w_dn = sb("w_dn", [P, EXPERTS, HALVES, 2, P], F32R)
        slot_gu = two("slot_gu", [P, 2, 2 * INNER], F32R)
        attn_raw = sb("attn_raw", [P, 4 * P])
        attn_hi = sb("attn_hi", [P, 3 * P], F32R)
        attn_lo = sb("attn_lo", [P, 3 * P], F32R)
        wo = attn_raw[:, 3 * P:4 * P]
        router_raw = sb("router_raw", [P, ROUTED])
        router_parts = sb("router_parts", [P, 2 * ROUTED], F32R)
        router_hi, router_lo = router_parts[:, 0:ROUTED], router_parts[:, ROUTED:2 * ROUTED]
        bias_b = sb("bias_b", [P, ROUTED])
        bq_col = sb("bq_col", [P, 1])
        bq_scaled = sb("bq_scaled", [P, 1])
        bv_b = sb("bv_b", [P, P])
        bo_b = sb("bo_b", [P, P])
        ident = sb("ident", [P, P])
        before = sb("before", [P, P], BF16)
        all_ones = sb("all_ones", [P, P], BF16)
        earlier = sb("earlier", [P, SUB, ROUTED, ROUTED], BF16)
        head_mask = sb("head_mask", [P, P])
        neg_half = sb("neg_half", [P, SUB])
        eps = sb("eps", [P, SUB])
        ones = sb("ones", [P, TT])
        widths = (tiles * PICKS * SUB, ROUTED, slots + 1, tiles, PICKS, SUB)
        starts = [sum(widths[:i]) for i in range(len(widths))]
        counting_i = sb("counting_i", [P, sum(widths)], I32)
        counting = sb("counting", [P, sum(widths)])

        def part(a, i):
            return a[:, starts[i]:starts[i] + widths[i]]

        def result_numbers(t):
            return part(counting, 0).rearrange("p (t n) -> p t n", t=tiles)[:, bass.ds(t, 1), :].rearrange(
                "p a (w s) -> p (a w) s", w=PICKS)

        region_start, slot_number, tile_rows, pick_number, nobody_numbers = [part(counting, i) for i in range(1, 6)]
        stats = sb("stats", [P, SUB, 6])
        mv = two("mv", [P, SUB, 2])
        var_eps = two("var_eps", [P, SUB])
        rstd = two("rstd", [P, SUB])
        shift = two("shift", [P, SUB])
        xn = two("xn", [P, SUB, P])
        xT_hi = two("xT_hi", [P, TT], F32R)
        xT_lo = two("xT_lo", [P, TT], F32R)
        send = two("send", [P, PICKS, SUB, ROW])
        send_to = two("send_to", [P, PICKS, SUB], I32)
        pad = sb("pad", [P, SUB, ROW])
        RW = SUB * ROUTED
        z_part = sb("z_part", [P, SUB, ROUTED])
        z = sb("z", [P, RW])
        z_square = sb("z_square", [P, RW])
        z_nudge = sb("z_nudge", [P, RW])
        z_safe = sb("z_safe", [P, RW])
        z_silu = sb("z_silu", [P, RW])
        z_recip = sb("z_recip", [P, RW])
        prob = sb("prob", [P, SUB, ROUTED])
        beaten = sb("beaten", [P, SUB, ROUTED, ROUTED], BF16)
        tied = sb("tied", [P, SUB, ROUTED, ROUTED], BF16)
        rank = sb("rank", [P, SUB, ROUTED])
        mask = sb("mask", [P, SUB + 1, ROUTED], BF16)
        pick = sb("pick", [P, PICKS, SUB, ROUTED])
        pick_prob = sb("pick_prob", [P, PICKS, SUB, ROUTED])
        score = sb("score", [P, PICKS, SUB])
        total = sb("total", [P, SUB])
        inv_total = sb("inv_total", [P, SUB])
        weight = sb("weight", [P, tiles, PICKS, SUB])
        filled = sb("filled", [P, ROUTED])
        place = sb("place", [P, SUB, ROUTED])
        pick_place = sb("pick_place", [P, PICKS, SUB, ROUTED])
        place_sum = sb("place_sum", [P, PICKS, SUB])
        SL = slots + 1
        count = sb("count", [1, ROUTED])
        over_rows = sb("over_rows", [1, ROUTED, tiles])
        n_slots = sb("n_slots", [1, ROUTED])
        n_before = sb("n_before", [1, ROUTED, ROUTED])
        slot_end = sb("slot_end", [1, ROUTED])
        passed = sb("passed", [1, SL, ROUTED])
        passed_n = sb("passed_n", [1, SL, ROUTED])
        slot_expert = sb("slot_expert", [1, SL])
        slot_start = sb("slot_start", [1, SL])
        slot_row = sb("slot_row", [1, SL])
        slot_w = sb("slot_w", [1, SL])
        row_table = sb("row_table", [1, SL], I32)
        w_table = sb("w_table", [1, SL], I32)
        pad_table = sb("pad_table", [1, ROUTED], I32)
        silu_g = two("silu_g", [P, TT])
        h = two("h", [P, TT])
        h_hi = [two(f"h_hi{i}_", [P, TT], F32R) for i in range(2)]
        h_lo = [two(f"h_lo{i}_", [P, TT], F32R) for i in range(2)]
        yT = sb("yT", [P, TT])
        y_rest = sb("y_rest", [P, SUB, P])
        y_out = two("y_out", [P, SUB, P])
        number = two("number", [P, SUB])
        placed = two("placed", [P, SUB])
        moved = sb("moved", [P, SUB])
        y_to = two("y_to", [P, SUB], I32)
        anchor = sb("anchor", [P, 1])
        y_in = [sb(f"y_in{i}", [P, SUB, PICKS, P]) for i in range(Y_RING)]
        q_silu = silu_g[0][:]
        k_silu = silu_g[1][:].rearrange("p (s d) -> p s d", s=SUB)
        phi_q = two("phi_q", [P, TT])
        phi_k = sb("phi_k", [P, SUB, P])
        v_sb = h[0][:].rearrange("p (s d) -> p s d", s=SUB)
        kv_sb = sb("kv_sb", [P, 2, P])
        kvo_sb = sb("kvo_sb", [P, 2, P])

        g_bank = [bank("g_bank0"), bank("g_bank1")]
        u_bank = [bank("u_bank0"), bank("u_bank1")]
        y_bank, tr_bank, tr_out, route_bank = bank("y_bank"), bank("tr_bank"), bank("tr_out"), bank("route_bank")
        row_bank = [y_bank, tr_out]
        q_bank, kv_bank = g_bank[0], u_bank[0]
        proj_bank = [g_bank[1], u_bank[1]]
        kvo_bank, att_bank = y_bank, tr_out

        x_first, x_some, x_rest = sem("x_first"), sem("x_some"), sem("x_rest")
        router_loaded, attn_loaded = sem("router_loaded"), sem("attn_loaded")
        w_loaded = [sem("w_loaded0"), sem("w_loaded1")]
        memsets, consts_ready, counted, pad_ready = sem("memsets"), sem("consts_ready"), sem("counted"), sem("pad_ready")
        counting_ready, earlier_ready = sem("counting_ready"), sem("earlier_ready")
        split_hi, split_lo = sem("split_hi"), sem("split_lo")
        split_dn = sem("split_dn")
        bq_ready = sem("bq_ready")
        stats_done, mv_done = sem("stats_done"), sem("mv_done")
        var_eps_done, rstd_done, shift_done = sem("var_eps_done"), sem("rstd_done"), sem("shift_done")
        xn_done = sem("xn_done")
        xT_psum, xT_hi_done, xT_lo_done = sem("xT_psum"), sem("xT_hi_done"), sem("xT_lo_done")
        logits_psum, route_step, z_silu_done = sem("logits_psum"), sem("route_step"), sem("z_silu_done")
        ranks_psum, send_done, filled_reset = sem("ranks_psum"), sem("send_done"), sem("filled_reset")
        sent = [sem("sent0"), sem("sent1")]
        table_step, padded, nobody_region = sem("table_step"), sem("padded"), sem("nobody_region")
        rows_loaded = [sem("rows_loaded0"), sem("rows_loaded1")]
        gu_loaded = [sem("gu_loaded0"), sem("gu_loaded1")]
        number_done, moved_done, placed_done = sem("number_done"), sem("moved_done"), sem("placed_done")
        y_to_done, anchored = sem("y_to_done"), sem("anchored")
        y_sent = [sem("y_sent0"), sem("y_sent1")]
        gu_psum, silu_done, h_done = sem("gu_psum"), sem("silu_done"), sem("h_done")
        h_hi_done, h_lo_done, down_done = sem("h_hi_done"), sem("h_lo_done"), sem("down_done")
        yT_done, y_psum, y_taken = sem("yT_done"), sem("y_psum"), sem("y_taken")
        y_rest_done = sem("y_rest_done")
        y_loaded = [sem(f"y_loaded{i}") for i in range(Y_RING)]
        first_added, both_added = sem("first_added"), sem("both_added")
        q_psum, proj_psum = sem("q_psum"), sem("proj_psum")
        q_silu_done, k_silu_done, v_done = sem("q_silu_done"), sem("k_silu_done"), sem("v_done")
        phi_q_done, phi_k_done, x_biased = sem("phi_q_done"), sem("phi_k_done"), sem("x_biased")
        kv_psum, kv_done, kvo_psum, kvo_done = sem("kv_psum"), sem("kv_done"), sem("kvo_psum"), sem("kvo_done")
        att_psum, x_attended = sem("att_psum"), sem("x_attended")
        stored = sem("stored")

        SPLIT_ROUTER, SPLIT_ATTN = 1, EXPERTS + 2
        TABLE_STEPS = 16

        def split_expert(e):
            return e + 2

        def x_tile(t):
            return x[:, bass.ds(t, 1), :].rearrange("p a n -> p (a n)")

        def x_sub(t, j):
            return x[:, bass.ds(t, 1), j * P:(j + 1) * P].rearrange("p a n -> p (a n)")

        def n_tile(f, t):
            return f * per_ffn + t

        def n_slot(f, s):
            return f * per_ffn + tiles + s

        def m_tile(f, t):
            return f * (per_ffn + tiles) + t

        def m_slot(f, s):
            return f * (per_ffn + tiles) + tiles + s

        def sent_count(f, i, each=SUB * PICKS * 16):
            return (f * TILES_OF + i.half + 1) * each

        def slot_count(f, i, each=16):
            return (f * SLOTS_OF[i.par] + i.half + 1) * each

        block = ctx.enter_context(nc.Block())

        @block.sync
        def _(sp):
            sp.dma_start(x[:, 0, :].rearrange("p (b n) -> p b n", b=2), x_view[0]).then_inc(x_first, 16)
            sp.dma_start(router_raw[:], router_wT).then_inc(router_loaded, 16)
            sp.dma_start(bias_b[:], routing_bias.partition_broadcast(P)).then_inc(router_loaded, 16)
            sp.dma_start(w_raw[0][:], w_experts[0]).then_inc(w_loaded[0], 16)
            for t in range(1, 4):
                sp.dma_start(x[:, t, :].rearrange("p (b n) -> p b n", b=2), x_view[t]).then_inc(x_some, 16)
            with sp.Fori(4, tiles) as t:
                sp.dma_start(x[:, bass.ds(t, 1), :].rearrange("p a (b n) -> p (a b) n", b=2),
                             x_view[bass.ds(t, 1)].rearrange("a p b n -> p (a b) n")).then_inc(x_rest, 16)
            sp.dma_start(attn_raw[:], w_attn).then_inc(attn_loaded, 16)
            sp.dma_start(bq_col[:], bq).then_inc(attn_loaded, 16)
            sp.dma_start(bv_b[:], bv.partition_broadcast(P)).then_inc(attn_loaded, 16)
            sp.dma_start(bo_b[:], bo.partition_broadcast(P)).then_inc(attn_loaded, 16)
            sp.wait_ge(pad_ready, 1)
            sp.dma_start(x_rows[ROUTED * region:ROUTED * region + TT].rearrange("(p j) d -> p j d", j=SUB),
                         pad[:]).then_inc(nobody_region, 16)

            def load_expert(i):
                sp.wait_ge(split_lo, i.t)
                sp.dma_start(w_raw[i.par][:], w_experts[bass.ds(i.t, 1)].rearrange("e p n -> p (e n)")
                             ).then_inc(w_loaded[i.par], 16)

            pairs(sp, 0, ROUTED // 2, load_expert)

            def load_rows(f, i):
                row = sp.value_load(row_table[0:1, bass.ds(i.t, 1)], min_val=0, max_val=ROUTED * region)
                if not i.is_(0, 1):
                    sp.wait_ge(number_done, f * slots + i.t - 1)
                sp.dma_start(send[i.par][:, 0], x_rows[bass.ds(row, TT)].rearrange("(p j) d -> p j d", j=SUB)
                             ).then_inc(rows_loaded[i.par], 16)

            def load_gate_up(f, i):
                e = sp.value_load(w_table[0:1, bass.ds(i.t, 1)], min_val=1, max_val=ROUTED)
                if not i.is_(0, 1):
                    sp.wait_ge(gu_psum, 2 * n_slot(f, i.t - 2) + 2)
                sp.dma_start(slot_gu[i.par][:].bitcast(F32).rearrange("p a n -> p (a n)"),
                             w_gu[:, bass.ds(e, 1)].bitcast(F32).rearrange("p e a n -> p (e a n)")
                             ).then_inc(gu_loaded[i.par], 16)

            def load_picks(t, slot, added):
                wait_count(sp, both_added, added)
                sp.dma_start(y_in[slot][:].rearrange("p (b j) w d -> p b (j w d)", b=2),
                             y_view[bass.ds(t, 1)].rearrange("a p b n -> p (a b) n")).then_inc(y_loaded[slot], 16)

            def store_tile(t):
                sp.wait_ge(both_added, t + (tiles + 1))
                sp.dma_start(out_view[bass.ds(t, 1)].rearrange("a p b n -> p (a b) n"),
                             x[:, bass.ds(t, 1), :].rearrange("p a (b n) -> p (a b) n", b=2)).then_inc(stored, 16)

            for f in range(2):
                sp.wait_ge(table_step, f * TABLE_STEPS + 1)
                for e in range(ROUTED):
                    end = sp.value_load(pad_table[0:1, e:e + 1], min_val=e * region, max_val=(e + 1) * region - TT)
                    sp.dma_start(x_rows[bass.ds(end, TT)].rearrange("(p j) d -> p j d", j=SUB),
                                 pad[:]).then_inc(padded, 16)
                if f == 0:
                    sp.wait_ge(split_lo, split_expert(ROUTED))
                sp.wait_ge(table_step, (f + 1) * TABLE_STEPS)
                load_gate_up(f, Ix(0))
                load_gate_up(f, Ix(1))
                sp.wait_ge(padded, (f + 1) * ROUTED * 16)
                sp.wait_ge(nobody_region, 16)
                sp.wait_ge(sent[0], sent_count(f, Ix(tiles - 2)))
                sp.wait_ge(sent[1], sent_count(f, Ix(tiles - 1)))
                load_rows(f, Ix(0))
                load_rows(f, Ix(1))

                def slot(i):
                    if not i.is_(slots - 2, slots - 1):
                        load_rows(f, i.at(2))
                        load_gate_up(f, i.at(2))

                over(sp, slots, slot, 2)
                sp.wait_ge(y_sent[0], slot_count(f, Ix(slots - 1), SUB * 16))
                sp.wait_ge(y_sent[1], slot_count(f, Ix(slots - 2), SUB * 16))
                if f == 0:
                    load_picks(0, 0, 0)
                    load_picks(1, 1, 0)

                    def ahead(i):
                        if not i.is_(tiles - 2, tiles - 1):
                            load_picks(i.t + 2, i.par, i.t + 1)

                    over(sp, tiles, ahead)
                else:
                    for t in range(Y_RING):
                        load_picks(t, t, tiles)
                    with sp.Fori(0, tiles // Y_RING - 1) as q:
                        for k in range(Y_RING):
                            t = q * Y_RING + k
                            store_tile(t)
                            load_picks(t + Y_RING, k, t + (tiles + 1))
                    for t in range(tiles - Y_RING, tiles):
                        store_tile(t)
            sp.wait_ge(stored, 16 * tiles)

        @block.gpsimd
        def _(pool):
            pool.iota(part(counting_i, 0), [[PICKS * TT, tiles], [1, PICKS], [PICKS * TT // 2, 2], [PICKS, 2]], base=0,
                      channel_multiplier=2 * PICKS).then_inc(counted, 1)
            pool.iota(part(counting_i, 1), [[region, ROUTED]], base=0, channel_multiplier=0).then_inc(counted, 1)
            pool.iota(part(counting_i, 2), [[1, slots + 1]], base=0, channel_multiplier=0).then_inc(counted, 1)
            pool.iota(part(counting_i, 3), [[TT, tiles]], base=0, channel_multiplier=0).then_inc(counted, 1)
            pool.iota(part(counting_i, 4), [[1, PICKS]], base=0, channel_multiplier=0).then_inc(counted, 1)
            pool.iota(part(counting_i, 5), [[1, SUB]], base=nobody, channel_multiplier=SUB).then_inc(counted, 1)
            pool.memset(neg_half[:], -0.5).then_inc(memsets, 1)
            pool.memset(eps[:], EPS).then_inc(memsets, 1)
            pool.memset(ident[:], 0.0).then_inc(memsets, 1)
            pool.wait_ge(memsets, 3)
            pool.affine_select(out=ident[:], in_=ident[:], compare_op=ALU.not_equal, fill=1.0, base=0,
                               pattern=[[-1, P]], channel_multiplier=1).then_inc(consts_ready, 1)

            def norm_scale(step, par):
                pool.wait_ge(mv_done, step + 1)
                pool.tensor_tensor(var_eps[par][:], mv[par][:, :, 1], eps[:], ALU.add).then_inc(var_eps_done, 1)
                pool.wait_ge(var_eps_done, step + 1)
                pool.tensor_tensor(rstd[par][:], var_eps[par][:], neg_half[:], ALU.pow).then_inc(rstd_done, 1)

            norm_scale(0, 0)
            norm_scale(1, 1)
            pool.memset(head_mask[:], 1.0).then_inc(memsets, 1)
            pool.memset(ones[:], 1.0).then_inc(memsets, 1)
            pool.memset(before[:], 1.0).then_inc(memsets, 1)
            pool.memset(all_ones[:], 1.0).then_inc(memsets, 1)
            pool.memset(anchor[:], 0.0).then_inc(memsets, 1)
            pool.wait_ge(memsets, 8)
            pool.affine_select(out=before[:], in_=before[:], compare_op=ALU.is_ge, fill=0.0, base=-1,
                               pattern=[[1, P]], channel_multiplier=-1).then_inc(consts_ready, 1)
            blocks = head_mask[:].rearrange("p (h d) -> p h d", d=HEAD)
            pool.affine_select(out=blocks, in_=blocks, compare_op=ALU.is_ge, fill=0.0, base=0,
                               pattern=[[-HEAD, HEADS], [0, HEAD]], channel_multiplier=1).then_inc(memsets, 1)
            pool.wait_ge(memsets, 9)
            pool.affine_select(out=blocks, in_=blocks, compare_op=ALU.is_ge, fill=0.0, base=HEAD - 1,
                               pattern=[[HEAD, HEADS], [0, HEAD]], channel_multiplier=-1).then_inc(consts_ready, 1)

            def anchor_waits(count):
                wait_count(pool, anchored, count)
                pool.tensor_tensor(anchor[:], eps[:, 0:1], eps[:, 0:1], ALU.add).then_inc(anchored, 1)

            ANCHORS = per_ffn

            def ffn_tile(f):
                def body(i):
                    r = f * tiles + i.t
                    if not i.is_(tiles - 2, tiles - 1):
                        norm_scale((FFN2 if f else FFN1) + i.t + 2, i.par)
                    pool.wait_ge(route_step, (r + 1) * ROUTE_STEPS)
                    pool.wait_ge(send_done, r + 1)
                    anchor_waits(f * ANCHORS + i.t)
                    for w in range(PICKS):
                        for j in range(SUB):
                            pool.indirect_dma_start(
                                x_rows, bass.IndirectOffsetOnAxis(ap=send_to[i.par][:, w, j:j + 1], axis=0),
                                send[i.par][:, w, j, :], None).then_inc(sent[i.par], 16)
                    if f == 0 and i.splits:
                        split_low(i.t, i.par)
                return body

            def slot_tile(f):
                def body(i):
                    pool.wait_ge(y_to_done, f * slots + i.t + 1)
                    pool.wait_ge(y_taken, n_slot(f, i.t) + 1)
                    anchor_waits(f * ANCHORS + tiles + i.t)
                    for j in range(SUB):
                        pool.indirect_dma_start(
                            y_rows, bass.IndirectOffsetOnAxis(ap=y_to[i.par][:, j:j + 1], axis=0),
                            y_out[i.par][:, j, :], None).then_inc(y_sent[i.par], 16)
                return body

            def attention_tile(i):
                pool.wait_ge(k_silu_done, i.t + 1)
                wait_count(pool, kv_psum, i.t)
                pool.tensor_tensor(phi_k[:].rearrange("p s d -> p (s d)"), silu_g[1][:], ones[:],
                                   ALU.add).then_inc(phi_k_done, 1)
                norm_scale(ATTN + i.t + 2, i.par)
                pool.wait_ge(q_silu_done, i.t + 1)
                pool.tensor_tensor(phi_q[i.par][:], q_silu, ones[:], ALU.add).then_inc(phi_q_done, 1)
                pool.wait_ge(xn_done, ATTN + i.t + 1)
                if i.is_(0):
                    pool.wait_ge(attn_loaded, 64)
                xt = x[:, bass.ds(i.t, 1), :].rearrange("p a (s d) -> p (a s) d", s=SUB)
                pool.tensor_tensor(xt, xt, bo_b[:].unsqueeze(1).to_broadcast([P, SUB, P]),
                                   ALU.add).then_inc(x_biased, 1)

            def split_low(e, par):
                pool.wait_ge(split_dn, e + 1)
                pool.tensor_tensor(w_gu[:, bass.ds(e, 1), 1, :].rearrange("p e n -> p (e n)"),
                                   w_raw[par][:, 0:2 * INNER],
                                   w_gu[:, bass.ds(e, 1), 0, :].bitcast(F32).rearrange("p e n -> p (e n)"),
                                   ALU.subtract).then_inc(split_lo, 1)

            over_tiles(pool, tiles, 0, ffn_tile(0))
            over(pool, slots, slot_tile(0), 2)
            norm_scale(ATTN, 0)
            norm_scale(ATTN + 1, 1)
            over(pool, tiles, attention_tile)
            over(pool, tiles, ffn_tile(1))
            over(pool, slots, slot_tile(1), 2)

        @block.scalar
        def _(act):
            def split_high(e, par, count):
                act.wait_ge(w_loaded[par], count)
                act.activation(w_gu[:, bass.ds(e, 1), 0, :].rearrange("p e n -> p (e n)"), w_raw[par][:, 0:2 * INNER],
                               ACT.Copy)
                act.activation(w_dn[:, bass.ds(e, 1), :, 0, :].rearrange("p e c n -> p (e c) n"),
                               w_raw[par][:, 2 * INNER:].rearrange("p (c n) -> p c n", c=HALVES),
                               ACT.Copy).then_inc(split_hi, 1)

            def xT_high(m, par):
                act.wait_ge(xT_psum, m + 1)
                act.activation(xT_hi[par][:], tr_bank[:], ACT.Copy).then_inc(xT_hi_done, 1)

            def normalise(step, t, par):
                act.wait_ge(shift_done, step + 1)
                for j in range(SUB):
                    last = act.activation(xn[par][:, j, :], x_sub(t, j), ACT.Identity, bias=shift[par][:, j:j + 1],
                                          scale=rstd[par][:, j:j + 1])
                last.then_inc(xn_done, 1)

            def silu(n, c):
                act.wait_ge(gu_psum, 2 * n + c + 1)
                wait_count(act, h_done, 2 * n + c - 1)
                act.activation(silu_g[c][:], g_bank[c][:], ACT.Silu).then_inc(silu_done, 1)

            def h_high(n, par, c):
                act.wait_ge(h_done, 2 * n + c + 1)
                wait_count(act, down_done, 2 * n + c - 3)
                act.activation(h_hi[par][c][:], h[c][:], ACT.Copy).then_inc(h_hi_done, 1)

            def y_evacuate(f, t):
                act.wait_ge(down_done, 2 * n_tile(f, t) + 2)
                wait_count(act, y_psum, f * tiles + t)
                act.activation(yT[:], y_bank[:], ACT.Copy).then_inc(yT_done, 1)

            def send_rows(f, i):
                act.wait_ge(xn_done, (FFN2 if f else FFN1) + i.t + 1)
                wait_count(act, sent[i.par], sent_count(f, i.at(-2)))
                act.activation(send[i.par][:, :, :, 0:P], xn[i.par][:].unsqueeze(1).to_broadcast([P, PICKS, SUB, P]),
                               ACT.Copy).then_inc(send_done, 1)

            def route_silu(r):
                act.wait_ge(route_step, r * ROUTE_STEPS + 5)
                act.activation(z_silu[:], z_safe[:], ACT.Silu).then_inc(z_silu_done, 1)

            def copy_rest(f, i):
                n = n_slot(f, i.t)
                act.wait_ge(down_done, 2 * n + 2)
                act.wait_ge(y_taken, n)
                for b in range(2):
                    last = act.activation(y_rest[:, 2 * b:2 * b + 2, :], row_bank[b][:].rearrange(
                        "p (j n) -> p j n", j=2)[:, :, P:2 * P], ACT.Copy)
                last.then_inc(y_rest_done, 1)

            def ffn_tile(f):
                def body(i):
                    n = n_tile(f, i.t)
                    last = i.is_(tiles - 1)
                    if not last:
                        xT_high(m_tile(f, i.t) + 1, 1 - i.par)
                    silu(n, 0)
                    if not last:
                        send_rows(f, i)
                    if f == 0 and i.splits:
                        split_high(i.t, i.par, (i.half + 1) * 16)
                    silu(n, 1)
                    h_high(n, i.par, 0)
                    h_high(n, i.par, 1)
                    if not i.is_(tiles - 2, tiles - 1):
                        act.wait_ge(send_done, f * tiles + i.t + 1)
                        normalise((FFN2 if f else FFN1) + i.t + 2, i.t + 2, i.par)
                    if not last:
                        route_silu(f * tiles + i.t + 1)
                    if not i.is_(0):
                        y_evacuate(f, i.t - 1)
                    if i.is_(tiles - 2):
                        send_rows(f, i.at(1))
                    if f == 0 and i.is_(tiles - 3):
                        act.wait_ge(attn_loaded, 64)
                        act.activation(attn_hi[:], attn_raw[:, 0:3 * P], ACT.Copy).then_inc(split_hi, 1)
                return body

            def slot_tile(f):
                def body(i):
                    n = n_slot(f, i.t)
                    if not i.is_(0):
                        h_high(n - 1, 1 - i.par, 1)
                    if not i.is_(slots - 1):
                        xT_high(m_slot(f, i.t) + 1, 1 - i.par)
                    if not i.is_(0, 1):
                        copy_rest(f, i.at(-2))
                    silu(n, 0)
                    silu(n, 1)
                    h_high(n, i.par, 0)
                    if i.is_(0):
                        y_evacuate(f, tiles - 1)
                return body

            def ffn(f):
                over_tiles(act, tiles, f, ffn_tile(f))
                xT_high(m_slot(f, 0), 0)
                over(act, slots, slot_tile(f), 2)
                n = n_slot(f, slots - 1)
                h_high(n, Ix(slots - 1).par, 1)
                copy_rest(f, Ix(slots - 2))
                copy_rest(f, Ix(slots - 1))

            def attention_tile(i):
                t = i.t
                act.wait_ge(proj_psum, t + 1)
                wait_count(act, phi_k_done, t)
                for b in range(2):
                    last = act.activation(k_silu[:, 2 * b:2 * b + 2, :], proj_bank[b][:].rearrange(
                        "p (j n) -> p j n", j=2)[:, :, 0:P], ACT.Silu, scale=SCALE)
                last.then_inc(k_silu_done, 1)
                xT_high(M_ATTN + t + 1, 1 - i.par)
                act.wait_ge(q_psum, t + 1)
                wait_count(act, phi_q_done, t)
                if i.is_(0):
                    act.wait_ge(bq_ready, 1)
                act.activation(q_silu, q_bank[:], ACT.Silu, bias=bq_scaled[:, 0:1],
                               scale=SCALE).then_inc(q_silu_done, 1)
                if not i.is_(0):
                    kvo_out(t - 1)
                normalise(ATTN + t + 2, t + 2 - tiles if i.is_(tiles - 2, tiles - 1) else t + 2, i.par)

            def kvo_out(t):
                act.wait_ge(kvo_psum, t + 1)
                wait_count(act, att_psum, t)
                act.activation(kvo_sb[:].rearrange("p b d -> p (b d)"), kvo_bank[:, 0:2 * P],
                               ACT.Copy).then_inc(kvo_done, 1)

            act.wait_ge(router_loaded, 32)
            act.activation(router_hi, router_raw[:], ACT.Copy).then_inc(split_hi, 1)
            normalise(0, 0, 0)
            xT_high(0, 0)
            split_high(0, 0, 16)
            normalise(1, 1, 1)
            route_silu(0)
            ffn(0)
            act.wait_ge(send_done, tiles)
            normalise(ATTN, 0, 0)
            xT_high(M_ATTN, 0)
            normalise(ATTN + 1, 1, 1)
            over(act, tiles, attention_tile)
            kvo_out(tiles - 1)
            route_silu(tiles)
            ffn(1)

        @block.tensor
        def _(pe):
            def three(bank_ap, w_parts, x_parts, start, stop):
                pe.matmul(bank_ap, w_parts[0], x_parts[0], start=start, stop=False)
                pe.matmul(bank_ap, w_parts[0], x_parts[1], start=False, stop=False)
                return pe.matmul(bank_ap, w_parts[1], x_parts[0], start=False, stop=stop)

            def transpose_in(m, src):
                wait_count(pe, xT_lo_done, m)
                for j in range(SUB):
                    last = pe.transpose(tr_bank[:, j * P:(j + 1) * P], src[:, j, 0:P], ident[:])
                last.then_inc(xT_psum, 1)

            def transpose_x(m, step, par):
                pe.wait_ge(xn_done, step + 1)
                transpose_in(m, xn[par])

            def transpose_rows(f, i):
                pe.wait_ge(rows_loaded[i.par], slot_count(f, i))
                transpose_in(m_slot(f, i.t), send[i.par][:, 0])

            def router(f, t, par):
                r = f * tiles + t
                pe.wait_ge(xT_lo_done, m_tile(f, t) + 1)
                if not (isinstance(r, int) and r == 0):
                    pe.wait_ge(route_step, (r - 1) * ROUTE_STEPS + PSUM_READ_STEP)
                for j in range(SUB):
                    s = slice(j * P, (j + 1) * P)
                    logits = route_bank[:, 2 * j * ROUTED:2 * (j + 1) * ROUTED]
                    pe.matmul(logits, xT_hi[par][:, s], router_parts[:], start=True, stop=False)
                    last = pe.matmul(logits, xT_lo[par][:, s], router_parts[:], start=False, stop=True)
                last.then_inc(logits_psum, 1)

            def ranks(r):
                pe.wait_ge(route_step, r * ROUTE_STEPS + MASK_STEP)
                out_ap = route_bank[:, RANKS]
                pe.matmul(out_ap, before[:], mask[:].rearrange("p s e -> p (s e)"), start=True, stop=False)
                for j in range(SUB):
                    last = pe.matmul(out_ap[:, (j + 1) * ROUTED:].rearrange("p (s e) -> p s e", e=ROUTED), all_ones[:],
                                     mask[:, j, :].unsqueeze(1).to_broadcast([P, SUB - j, ROUTED]),
                                     start=False, stop=(j == SUB - 1))
                last.then_inc(ranks_psum, 1)

            def gate_up(n, c, par, w):
                wait_count(pe, h_done, 2 * n + c - 1)
                xs = (xT_hi[par][:], xT_lo[par][:])
                g, u = slice(c * P, (c + 1) * P), slice(INNER + c * P, INNER + (c + 1) * P)
                three(g_bank[c][:], (w[:, 0, g], w[:, 1, g]), xs, True, True)
                three(u_bank[c][:], (w[:, 0, u], w[:, 1, u]), xs, True, True).then_inc(gu_psum, 1)

            def down_shared(f, t, t_par):
                n = n_tile(f, t)
                for c in range(HALVES):
                    pe.wait_ge(h_lo_done, 2 * n + c + 1)
                    if c == 0:
                        wait_count(pe, yT_done, f * tiles + t)
                    three(y_bank[:], (w_dn[:, 0, c, 0, :], w_dn[:, 0, c, 1, :]), (h_hi[t_par][c][:], h_lo[t_par][c][:]), c == 0,
                          c == HALVES - 1).then_inc(down_done, 1)

            def down_rows(f, i):
                n = n_slot(f, i.t)
                e = pe.value_load(w_table[0:1, bass.ds(i.t, 1)], min_val=1, max_val=ROUTED)
                pe.wait_ge(h_lo_done, 2 * n + 2)
                if i.is_(0):
                    pe.wait_ge(yT_done, (f + 1) * tiles)
                pe.wait_ge(y_taken, n)
                for j in range(SUB):
                    s = slice(j * P, (j + 1) * P)
                    rows = row_bank[j // 2][:, (j % 2) * 2 * P:(j % 2 + 1) * 2 * P]
                    for c in range(HALVES):
                        w = w_dn[:, bass.ds(e, 1), c, :, :].rearrange("p e a n -> p (e a n)")
                        pe.matmul(rows, h_hi[i.par][c][:, s], w, start=(c == 0), stop=False)
                        last = pe.matmul(rows, h_lo[i.par][c][:, s], w, start=False, stop=(c == HALVES - 1))
                last.then_inc(down_done, 2)

            def transpose_y(f, t):
                n = n_tile(f, t)
                pe.wait_ge(yT_done, f * tiles + t + 1)
                wait_count(pe, y_taken, n)
                for j in range(SUB):
                    last = pe.transpose(tr_out[:, j * P:(j + 1) * P], yT[:, j * P:(j + 1) * P], ident[:])
                last.then_inc(y_psum, 1)

            shared_gu = w_gu[:, 0]

            def ffn_tile(f):
                def body(i):
                    n, m = n_tile(f, i.t), m_tile(f, i.t)
                    step = (FFN2 if f else FFN1) + i.t
                    last = i.is_(tiles - 1)
                    if not last:
                        transpose_x(m + 1, step + 1, 1 - i.par)
                    pe.wait_ge(xT_lo_done, m + 1)
                    if f == 0 and i.is_(0):
                        pe.wait_ge(split_lo, split_expert(0))
                    gate_up(n, 0, i.par, shared_gu)
                    if not last:
                        ranks(f * tiles + i.t)
                    if not i.is_(0, 1):
                        transpose_y(f, i.t - 2)
                    gate_up(n, 1, i.par, shared_gu)
                    if not last:
                        router(f, i.t + 1, 1 - i.par)
                    if not i.is_(0):
                        down_shared(f, i.t - 1, 1 - i.par)
                    if i.is_(tiles - 2):
                        ranks(f * tiles + tiles - 1)
                return body

            def slot_tile(f):
                def body(i):
                    n = n_slot(f, i.t)
                    if not i.is_(slots - 1):
                        transpose_rows(f, i.at(1))
                    pe.wait_ge(xT_lo_done, m_slot(f, i.t) + 1)
                    pe.wait_ge(gu_loaded[i.par], slot_count(f, i))
                    gate_up(n, 0, i.par, slot_gu[i.par])
                    if i.is_(0, 1):
                        transpose_y(f, tiles - 2 + i.t)
                    gate_up(n, 1, i.par, slot_gu[i.par])
                    if i.is_(0):
                        down_shared(f, tiles - 1, 1)
                    else:
                        down_rows(f, i.at(-1))
                return body

            def ffn(f):
                over(pe, tiles, ffn_tile(f))
                transpose_rows(f, Ix(0))
                over(pe, slots, slot_tile(f), 2)
                down_rows(f, Ix(slots - 1))

            def attention_tile(i):
                t, par = i.t, i.par
                pe.wait_ge(xT_lo_done, M_ATTN + t + 1)
                wait_count(pe, k_silu_done, t)
                wait_count(pe, v_done, t)
                for j in range(SUB):
                    s = slice(j * P, (j + 1) * P)
                    last = three(proj_bank[j // 2][:, (j % 2) * 2 * P:(j % 2 + 1) * 2 * P],
                                 (xT_hi[par][:, s], xT_lo[par][:, s]),
                                 (attn_hi[:, P:3 * P], attn_lo[:, P:3 * P]), True, True)
                last.then_inc(proj_psum, 1)
                transpose_x(M_ATTN + t + 1, ATTN + t + 1, 1 - par)
                if not i.is_(0):
                    key_value(t - 1)
                wait_count(pe, q_silu_done, t)
                three(q_bank[:], (attn_hi[:, 0:P], attn_lo[:, 0:P]), (xT_hi[par][:], xT_lo[par][:]),
                      True, True).then_inc(q_psum, 1)
                if not i.is_(0):
                    times_wo(t - 1)
                if not i.is_(0):
                    attend(t - 1, 1 - par)

            def key_value(t):
                pe.wait_ge(phi_k_done, t + 1)
                pe.wait_ge(v_done, t + 1)
                wait_count(pe, kv_done, t)
                for b in range(2):
                    for j in range(2):
                        last = pe.matmul(kv_bank[:, b * P:(b + 1) * P], v_sb[:, 2 * b + j, :],
                                         phi_k[:, 2 * b + j, :], start=(j == 0), stop=(j == 1))
                last.then_inc(kv_psum, 1)

            def times_wo(t):
                pe.wait_ge(kv_done, t + 1)
                wait_count(pe, kvo_done, t)
                for b in range(2):
                    last = pe.matmul(kvo_bank[:, b * P:(b + 1) * P], kv_sb[:, b, :], wo, start=True, stop=True)
                last.then_inc(kvo_psum, 1)

            def attend(t, par):
                pe.wait_ge(kvo_done, t + 1)
                pe.wait_ge(phi_q_done, t + 1)
                wait_count(pe, x_attended, t)
                for j in range(SUB):
                    last = pe.matmul(att_bank[:, j * P:(j + 1) * P], phi_q[par][:, j * P:(j + 1) * P],
                                     kvo_sb[:, j // 2, :], start=True, stop=True)
                last.then_inc(att_psum, 1)

            pe.wait_ge(consts_ready, 1)
            transpose_x(0, 0, 0)
            pe.wait_ge(split_lo, SPLIT_ROUTER)
            router(0, 0, 0)
            pe.wait_ge(consts_ready, 2)
            ffn(0)
            pe.wait_ge(y_taken, per_ffn)
            pe.wait_ge(split_lo, SPLIT_ATTN)
            transpose_x(M_ATTN, ATTN, 0)
            over(pe, tiles, attention_tile)
            router(1, 0, 0)
            key_value(tiles - 1)
            times_wo(tiles - 1)
            attend(tiles - 1, 1)
            pe.wait_ge(x_attended, tiles)
            ffn(1)

        @block.vector
        def _(dve):
            def split_low(e, par):
                split_down_low(e, par)
                dve.tensor_tensor(w_gu[:, bass.ds(e, 1), 1, :].rearrange("p e n -> p (e n)"),
                                  w_raw[par][:, 0:2 * INNER],
                                  w_gu[:, bass.ds(e, 1), 0, :].bitcast(F32).rearrange("p e n -> p (e n)"),
                                  ALU.subtract).then_inc(split_lo, 1)

            def split_down_low(e, par):
                dve.wait_ge(split_hi, split_expert(e))
                hi, lo = [w_dn[:, bass.ds(e, 1), :, part_, :].rearrange("p e c n -> p (e c) n") for part_ in range(2)]
                dve.tensor_tensor(lo, w_raw[par][:, 2 * INNER:].rearrange("p (c n) -> p c n", c=HALVES),
                                  hi.bitcast(F32), ALU.subtract).then_inc(split_dn, 1)

            def norm_stats(t, j):
                op = dve.bn_stats(stats[:, j, :], x_sub(t, j))
                if j == SUB - 1:
                    op.then_inc(stats_done, 1)

            def norm_mean(par):
                for j in range(SUB):
                    last = dve.bn_aggr(mv[par][:, j, :], stats[:, j, :])
                last.then_inc(mv_done, 1)

            def norm_shift(step, par):
                dve.wait_ge(mv_done, step + 1)
                dve.wait_ge(rstd_done, step + 1)
                dve.scalar_tensor_tensor(out=shift[par][:], in0=mv[par][:, :, 0], scalar=-1.0, in1=rstd[par][:],
                                         op0=ALU.mult, op1=ALU.mult).then_inc(shift_done, 1)

            def xT_low(m, par):
                dve.wait_ge(xT_hi_done, m + 1)
                dve.tensor_tensor(xT_lo[par][:], tr_bank[:], xT_hi[par][:].bitcast(F32),
                                  ALU.subtract).then_inc(xT_lo_done, 1)

            def multiply(n, c):
                dve.wait_ge(silu_done, 2 * n + c + 1)
                wait_count(dve, h_lo_done, 2 * n + c - 1)
                dve.tensor_tensor(h[c][:], silu_g[c][:], u_bank[c][:], ALU.mult).then_inc(h_done, 1)

            def h_low(n, par, c):
                dve.wait_ge(h_hi_done, 2 * n + c + 1)
                dve.tensor_tensor(h_lo[par][c][:], h[c][:], h_hi[par][c][:].bitcast(F32),
                                  ALU.subtract).then_inc(h_lo_done, 1)

            def add_shared(f, t):
                dve.wait_ge(y_psum, f * tiles + t + 1)
                dve.scalar_tensor_tensor(out=x_tile(t), in0=tr_out[:], scalar=0.5, in1=x_tile(t), op0=ALU.mult,
                                         op1=ALU.add).then_inc(y_taken, 1)

            def route(f, i, steps):
                r = f * tiles + i.t
                all_experts = [P, SUB, ROUTED, ROUTED]
                both = [P, PICKS, SUB, ROUTED]
                other = prob[:].unsqueeze(2).to_broadcast(all_experts)
                logits = route_bank[:, LOGITS].rearrange("p (j n) -> p j n", n=2 * ROUTED)
                own = prob[:].unsqueeze(3).to_broadcast(all_experts)
                for n in steps:
                    if n > 0:
                        dve.wait_ge(route_step, r * ROUTE_STEPS + n)
                    if n == 0:
                        dve.wait_ge(logits_psum, r + 1)
                        op = dve.tensor_tensor(z_part[:], logits[:, :, 0:ROUTED],
                                               bias_b[:].unsqueeze(1).to_broadcast([P, SUB, ROUTED]), ALU.add)
                    if n == 1:
                        op = dve.tensor_tensor(z[:].rearrange("p (j e) -> p j e", e=ROUTED), z_part[:],
                                               logits[:, :, ROUTED:], ALU.add)
                    if n == 2:
                        op = dve.tensor_tensor(z_square[:], z[:], z[:], ALU.mult)
                    if n == 3:
                        op = dve.tensor_scalar(z_nudge[:], z_square[:], 1e-36, 2e-18, ALU.is_lt, ALU.mult)
                    if n == 4:
                        op = dve.tensor_tensor(z_safe[:], z[:], z_nudge[:], ALU.add)
                    if n == 5:
                        op = dve.reciprocal(z_recip[:], z_safe[:])
                    if n == 6:
                        dve.wait_ge(z_silu_done, r + 1)
                        op = dve.tensor_tensor(prob[:].rearrange("p j e -> p (j e)"), z_silu[:], z_recip[:], ALU.mult)
                    if n == 7:
                        op = dve.tensor_tensor(beaten[:], other, own, ALU.is_gt)
                    if n == 8:
                        op = dve.tensor_tensor(tied[:], other, own, ALU.is_equal)
                    if n == 9:
                        op = dve.tensor_tensor(tied[:], tied[:], earlier[:], ALU.mult)
                    if n == 10:
                        op = dve.tensor_tensor(beaten[:], beaten[:], tied[:], ALU.add)
                    if n == 11:
                        op = dve.tensor_reduce(rank[:], beaten[:], AX_X, ALU.add)
                    if n == 12:
                        op = dve.tensor_scalar(mask[:, 0:SUB, :], rank[:], PICKS - 0.5, None, ALU.is_lt)
                    if n == 13:
                        op = dve.tensor_tensor(pick[:], rank[:].unsqueeze(1).to_broadcast(both),
                                               pick_number.unsqueeze(2).unsqueeze(3).to_broadcast(both), ALU.is_equal)
                    if n == 14:
                        op = dve.tensor_tensor(pick_prob[:], pick[:], prob[:].unsqueeze(1).to_broadcast(both), ALU.mult)
                    if n == 15:
                        op = dve.tensor_reduce(score[:], pick_prob[:], AX_X, ALU.add)
                    if n == 16:
                        op = dve.tensor_tensor(total[:], score[:, 0, :], score[:, 1, :], ALU.add)
                    if n == 17:
                        op = dve.reciprocal(inv_total[:], total[:])
                    if n == 18:
                        op = dve.scalar_tensor_tensor(
                            out=weight[:, bass.ds(i.t, 1), :, :].rearrange("p a w s -> p (a w) s"), in0=score[:],
                            scalar=0.5, in1=inv_total[:].unsqueeze(1).to_broadcast([P, PICKS, SUB]),
                            op0=ALU.mult, op1=ALU.mult)
                    if n == 19:
                        dve.wait_ge(ranks_psum, r + 1)
                        if i.is_(0):
                            dve.wait_ge(filled_reset, f + 1)
                        op = dve.tensor_tensor(place[:], route_bank[:, RANKS][:, 0:RW].rearrange(
                            "p (j e) -> p j e", e=ROUTED), filled[:].unsqueeze(1).to_broadcast([P, SUB, ROUTED]), ALU.add)
                    if n == 20:
                        op = dve.tensor_tensor(filled[:], filled[:], route_bank[:, RANKS][:, RW:RW + ROUTED], ALU.add)
                    if n == 21:
                        op = dve.tensor_tensor(pick_place[:], pick[:], place[:].unsqueeze(1).to_broadcast(both), ALU.mult)
                    if n == 22:
                        op = dve.tensor_reduce(place_sum[:], pick_place[:], AX_X, ALU.add)
                    if n == 23:
                        wait_count(dve, sent[i.par], sent_count(f, i.at(-2)))
                        op = dve.tensor_copy(send_to[i.par][:], place_sum[:])
                    if n == 24:
                        op = dve.tensor_scalar(send[i.par][:, :, :, P], result_numbers(i.t), 0.0, None, ALU.add)
                    op.then_inc(route_step, 1)

            def slot_table(f):
                grid = [1, SL, ROUTED]
                dve.wait_ge(route_step, (f + 1) * tiles * ROUTE_STEPS)
                for n in range(TABLE_STEPS):
                    if n > 0:
                        dve.wait_ge(table_step, f * TABLE_STEPS + n)
                    if n == 0:
                        op = dve.tensor_copy(pad_table[:], filled[0:1, :])
                    if n == 1:
                        op = dve.tensor_tensor(count[:], filled[0:1, :], region_start[0:1, :], ALU.subtract)
                    if n == 2:
                        op = dve.tensor_tensor(over_rows[:], count[:].unsqueeze(2).to_broadcast([1, ROUTED, tiles]),
                                               tile_rows[0:1, :].unsqueeze(1).to_broadcast([1, ROUTED, tiles]), ALU.is_gt)
                    if n == 3:
                        op = dve.tensor_reduce(n_slots[:], over_rows[:], AX_X, ALU.add)
                    if n == 4:
                        op = dve.tensor_tensor(n_before[:], n_slots[:].unsqueeze(1).to_broadcast([1, ROUTED, ROUTED]),
                                               earlier[0:1, 0, :, :], ALU.mult)
                    if n == 5:
                        op = dve.tensor_reduce(slot_end[:], n_before[:], AX_X, ALU.add)
                    if n == 6:
                        op = dve.tensor_tensor(slot_end[:], slot_end[:], n_slots[:], ALU.add)
                    if n == 7:
                        op = dve.tensor_tensor(passed[:], slot_end[:].unsqueeze(1).to_broadcast(grid),
                                               slot_number[0:1, :].unsqueeze(2).to_broadcast(grid), ALU.is_le)
                    if n == 8:
                        op = dve.tensor_reduce(slot_expert[:], passed[:], AX_X, ALU.add)
                    if n == 9:
                        op = dve.tensor_tensor(passed_n[:], passed[:], n_slots[:].unsqueeze(1).to_broadcast(grid), ALU.mult)
                    if n == 10:
                        op = dve.tensor_reduce(slot_start[:], passed_n[:], AX_X, ALU.add)
                    if n == 11:
                        op = dve.tensor_tensor(slot_row[:], slot_number[0:1, :], slot_start[:], ALU.subtract)
                    if n == 12:
                        op = dve.tensor_scalar(slot_row[:], slot_row[:], float(TT), None, ALU.mult)
                    if n == 13:
                        op = dve.scalar_tensor_tensor(out=slot_row[:], in0=slot_expert[:], scalar=float(region),
                                                      in1=slot_row[:], op0=ALU.mult, op1=ALU.add)
                    if n == 14:
                        op = dve.tensor_scalar(row_table[:], slot_row[:], float(ROUTED * region), None, ALU.min)
                    if n == 15:
                        op = dve.tensor_scalar(w_table[:], slot_expert[:], float(ROUTED - 1), 1.0, ALU.min, ALU.add)
                    op.then_inc(table_step, 1)

            def add_first(f, t, slot, loads):
                dve.wait_ge(y_loaded[slot], loads * 16)
                add_pick(t, slot, 0).then_inc(first_added, 1)

            def add_second(f, t, slot):
                dve.wait_ge(first_added, t + (f * tiles + 1))
                add_pick(t, slot, 1).then_inc(both_added, 1)

            def add_pick(t, slot, w):
                for j in range(SUB):
                    last = dve.scalar_tensor_tensor(
                        out=x_sub(t, j), in0=y_in[slot][:, j, w, :],
                        scalar=weight[:, bass.ds(t, 1), w, j:j + 1].rearrange("p a s -> p (a s)"),
                        in1=x_sub(t, j), op0=ALU.mult, op1=ALU.add)
                return last

            def ffn_tile(f):
                def body(i):
                    t, par = i.t, i.par
                    n, m = n_tile(f, t), m_tile(f, t)
                    first, last = i.is_(0), i.is_(tiles - 1)
                    norm = not i.is_(tiles - 2, tiles - 1)
                    step = (FFN2 if f else FFN1) + t + 2
                    here = () if last else range(LATE, ROUTE_STEPS)
                    ahead = i.at(1)

                    def later(*steps):
                        route(f, i, [LATE + s for s in steps if LATE + s in here])

                    if not last:
                        xT_low(m + 1, 1 - par)
                    for j in range(SUB):
                        if norm:
                            if f == 0 and j == 0 and i.is_(2):
                                dve.wait_ge(x_rest, 16 * (tiles - 4))
                            norm_stats(t + 2, j)
                        later(j)
                    if norm:
                        dve.wait_ge(stats_done, step + 1)
                        dve.wait_ge(xn_done, step - 1)
                    if not first:
                        h_low(n - 1, 1 - par, 0)
                    later(4)
                    if norm:
                        norm_mean(par)
                    later(5, 6)
                    if not first:
                        h_low(n - 1, 1 - par, 1)
                    later(7)
                    if f == 0 and i.splits:
                        split_down_low(t, par)
                    multiply(n, 0)
                    later(8, 9)
                    multiply(n, 1)
                    if norm:
                        norm_shift(step, par)
                    later(10, 11)
                    if not last:
                        route(f, ahead, [0])
                    if not last:
                        route(f, ahead, [1])
                    if not last:
                        route(f, ahead, range(2, 6))
                    if not i.is_(0, 1):
                        add_shared(f, t - 2)
                    if not last:
                        route(f, ahead, range(6, LATE))
                    if i.is_(tiles - 2):
                        route(f, ahead, range(LATE, ROUTE_STEPS))
                        slot_table(f)
                    if f == 0 and i.is_(tiles - 3):
                        dve.wait_ge(split_hi, SPLIT_ATTN)
                        dve.tensor_tensor(attn_lo[:], attn_raw[:, 0:3 * P], attn_hi[:].bitcast(F32),
                                          ALU.subtract).then_inc(split_lo, 1)
                        dve.tensor_scalar(bq_scaled[:], bq_col[:], SCALE, None, ALU.mult).then_inc(bq_ready, 1)
                return body

            def copy_number(f, i):
                k = f * slots + i.t
                dve.wait_ge(rows_loaded[i.par], slot_count(f, i))
                wait_count(dve, placed_done, k - 1)
                dve.tensor_copy(number[i.par][:], send[i.par][:, 0, :, P]).then_inc(number_done, 1)

            def place_results(f, i):
                k = f * slots + i.t
                dve.wait_ge(number_done, k + 1)
                wait_count(dve, y_to_done, k - 1)
                if i.par:
                    dve.tensor_scalar(moved[:], number[1][:], float(nobody), float(TT), ALU.is_ge,
                                      ALU.mult).then_inc(moved_done, 1)
                    dve.wait_ge(moved_done, f * SLOTS_OF[1] + i.half + 1)
                    dve.tensor_tensor(placed[1][:], moved[:], number[1][:], ALU.add).then_inc(placed_done, 1)
                else:
                    dve.tensor_copy(placed[0][:], number[0][:]).then_inc(placed_done, 1)

            def place_numbers(f, i):
                dve.wait_ge(placed_done, f * slots + i.t + 1)
                wait_count(dve, y_sent[i.par], slot_count(f, i.at(-2), SUB * 16))
                dve.tensor_copy(y_to[i.par][:], placed[i.par][:]).then_inc(y_to_done, 1)

            def add_halves(f, i):
                n = n_slot(f, i.t)
                dve.wait_ge(y_rest_done, f * slots + i.t + 1)
                wait_count(dve, y_sent[i.par], slot_count(f, i.at(-2), SUB * 16))
                for b in range(2):
                    js = slice(2 * b, 2 * b + 2)
                    last = dve.tensor_tensor(y_out[i.par][:, js, :], row_bank[b][:].rearrange(
                        "p (j n) -> p j n", j=2)[:, :, 0:P], y_rest[:, js, :], ALU.add)
                last.then_inc(y_taken, 1)

            def slot_tile(f):
                def body(i):
                    n = n_slot(f, i.t)
                    h_low(n - 1, 1 - i.par, 0)
                    h_low(n - 1, 1 - i.par, 1)
                    if not i.is_(0):
                        place_results(f, i.at(-1))
                    if not i.is_(slots - 1):
                        xT_low(m_slot(f, i.t) + 1, 1 - i.par)
                        copy_number(f, i.at(1))
                    if i.is_(0, 1):
                        add_shared(f, tiles - 2 + i.t)
                    else:
                        place_numbers(f, i.at(-2))
                        add_halves(f, i.at(-2))
                    multiply(n, 0)
                    multiply(n, 1)
                return body

            def ffn(f):
                over_tiles(dve, tiles, f, ffn_tile(f))
                xT_low(m_slot(f, 0), 0)
                copy_number(f, Ix(0))
                over(dve, slots, slot_tile(f), 2)
                i = Ix(slots - 1)
                h_low(n_slot(f, i.t), i.par, 0)
                h_low(n_slot(f, i.t), i.par, 1)
                place_results(f, i)
                for k in (i.at(-1), i):
                    place_numbers(f, k)
                    add_halves(f, k)

            def attention_tile(i):
                t, par = i.t, i.par
                step = ATTN + t + 2
                nt = t + 2 - tiles if i.is_(tiles - 2, tiles - 1) else t + 2
                picks = not i.is_(tiles - 3, tiles - 2, tiles - 1)
                if not picks and nt < 2:
                    dve.wait_ge(x_attended, nt + 1)
                for j in range(SUB):
                    norm_stats(nt, j)
                if picks:
                    add_first(0, t + 3, 1 - par, i.at(3).half + 1)
                dve.wait_ge(stats_done, step + 1)
                dve.wait_ge(xn_done, step - 1)
                xT_low(M_ATTN + t + 1, 1 - par)
                norm_mean(par)
                if not i.is_(0):
                    mask_heads(t - 1)
                if picks:
                    add_second(0, t + 3, 1 - par)
                norm_shift(step, par)
                if picks:
                    dve.wait_ge(both_added, t + 4)
                dve.wait_ge(k_silu_done, t + 1)
                wait_count(dve, kv_psum, t)
                for b in range(2):
                    last = dve.tensor_tensor(v_sb[:, 2 * b:2 * b + 2, :], proj_bank[b][:].rearrange(
                        "p (j n) -> p j n", j=2)[:, :, P:2 * P], bv_b[:].unsqueeze(1).to_broadcast([P, 2, P]), ALU.add)
                last.then_inc(v_done, 1)
                if not i.is_(0):
                    add_attention(t - 1)

            def mask_heads(t):
                dve.wait_ge(kv_psum, t + 1)
                wait_count(dve, kvo_psum, t)
                dve.tensor_tensor(kv_sb[:], kv_bank[:, 0:2 * P].rearrange("p (b d) -> p b d", b=2),
                                  head_mask[:].unsqueeze(1).to_broadcast([P, 2, P]), ALU.mult).then_inc(kv_done, 1)

            def add_attention(t):
                dve.wait_ge(att_psum, t + 1)
                dve.wait_ge(x_biased, t + 1)
                dve.tensor_tensor(x_tile(t), att_bank[:], x_tile(t), ALU.add).then_inc(x_attended, 1)

            dve.wait_ge(x_first, 16)
            for j in range(SUB):
                norm_stats(0, j)
            dve.wait_ge(stats_done, 1)
            norm_mean(0)
            dve.wait_ge(mv_done, 1)
            dve.wait_ge(x_some, 48)
            for j in range(SUB):
                norm_stats(1, j)
            dve.wait_ge(stats_done, 2)
            norm_mean(1)
            dve.memset(earlier[:], 0.0).then_inc(earlier_ready, 1)
            dve.memset(mask[:], 0.0).then_inc(earlier_ready, 1)
            dve.memset(pad[:], 0.0).then_inc(earlier_ready, 1)
            norm_shift(0, 0)
            dve.wait_ge(earlier_ready, 3)
            for e in range(1, ROUTED):
                last_set = dve.memset(earlier[:, :, e, 0:e], 1.0)
            last_set.then_inc(earlier_ready, 1)
            dve.wait_ge(counted, 6)
            dve.tensor_copy(counting[:], counting_i[:]).then_inc(counting_ready, 1)
            dve.wait_ge(split_hi, SPLIT_ROUTER)
            dve.tensor_tensor(router_lo, router_raw[:], router_hi.bitcast(F32),
                              ALU.subtract).then_inc(split_lo, 1)
            xT_low(0, 0)
            split_low(0, 0)
            norm_shift(1, 1)
            dve.wait_ge(counting_ready, 1)
            dve.tensor_copy(pad[:, :, P], nobody_numbers).then_inc(pad_ready, 1)
            dve.tensor_copy(filled[:], region_start).then_inc(filled_reset, 1)
            dve.wait_ge(earlier_ready, 4)
            route(0, Ix(0), range(LATE))
            ffn(0)
            dve.wait_ge(consts_ready, 3)
            def stats_of(t):
                dve.wait_ge(both_added, t + 1)
                for j in range(SUB):
                    norm_stats(t, j)
                dve.wait_ge(stats_done, ATTN + t + 1)
                norm_mean(t)

            add_first(0, 0, 0, 1)
            add_second(0, 0, 0)
            stats_of(0)
            add_first(0, 1, 1, 1)
            norm_shift(ATTN, 0)
            add_second(0, 1, 1)
            stats_of(1)
            xT_low(M_ATTN, 0)
            norm_shift(ATTN + 1, 1)
            add_first(0, 2, 0, 2)
            add_second(0, 2, 0)
            dve.wait_ge(both_added, 3)
            over(dve, tiles, attention_tile)
            mask_heads(tiles - 1)
            dve.wait_ge(table_step, TABLE_STEPS)
            dve.tensor_copy(filled[:], region_start).then_inc(filled_reset, 1)
            route(1, Ix(0), range(6))
            add_attention(tiles - 1)
            route(1, Ix(0), range(6, LATE))
            ffn(1)
            before_end = [tiles // 2, tiles // 2, 0, 0]
            add_first(1, 0, 0, before_end[0] + 1)

            def picks_of(q, quarters):
                for k in range(Y_RING):
                    k_next, q_next = (k + 1) % Y_RING, q + (k + 1) // Y_RING
                    if not (isinstance(q, int) and q_next == quarters):
                        add_first(1, q * Y_RING + k + 1, k_next, q_next + before_end[k_next] + 1)
                    add_second(1, q * Y_RING + k, k)

            with dve.Fori(0, tiles // Y_RING - 1) as q:
                picks_of(q, tiles // Y_RING)
            picks_of(tiles // Y_RING - 1, tiles // Y_RING)



_OUT = ((32, 256, 128), "float32")


def kernel(**inputs):
    import numpy as np
    import concourse.bacc as bacc
    from concourse.bass_utils import run_bass_kernel_spmd

    a = {k: np.asarray(v) for k, v in inputs.items()}
    gate = np.concatenate([a["L0_ffn_shared_gate"].T[None], a["L0_ffn_gate_w"]])
    up = np.concatenate([a["L0_ffn_shared_up"].T[None], a["L0_ffn_up_w"]])
    down = np.concatenate([a["L0_ffn_shared_down"].T[None], a["L0_ffn_down_w"]])
    arrays = {
        "x_in": a["L0_attn_x"].reshape(-1, P),
        "w_experts": np.concatenate([gate, up, down[:, :P], down[:, P:]], axis=2),
        "router_wT": a["L0_ffn_router_w"].T,
        "routing_bias": a["L0_ffn_routing_bias"],
        "w_attn": np.concatenate([a["L0_attn_" + n].T for n in ("Wq", "Wk", "Wv", "Wo")], axis=1),
        "bq": a["L0_attn_bq"].reshape(P, 1),
        "bv": a["L0_attn_bv"],
        "bo": a["L0_attn_bo"],
    }
    arrays = {k: np.ascontiguousarray(v) for k, v in arrays.items()}
    nc = bacc.Bacc("TRN2", target_bir_lowering=False, num_devices=1)
    args = [nc.dram_tensor(k, v.shape, mybir.dt.from_np(v.dtype), kind="ExternalInput").ap() for k, v in arrays.items()]
    out = nc.dram_tensor("out", (a["L0_attn_x"].size // P, P), F32, kind="ExternalOutput").ap()
    macaron(nc, *args, out)
    result = run_bass_kernel_spmd(nc, [arrays], core_ids=[0])
    return result.results[0]["out"].reshape(_OUT[0])
```
